# Optimizing a Trainium2 kernel written in Bass

```python
import numpy as np
import jax
import jax.numpy as jnp

def _softmax(x, axis=-1):
    return jax.nn.softmax(x, axis=axis)

def _gelu(x):
    return jax.nn.gelu(x, approximate=True)

def _silu(x):
    return jax.nn.silu(x)

def _sigmoid(x):
    return jax.nn.sigmoid(x)

def _layernorm(x, axis=-1, eps=1e-05):
    m = jnp.mean(x, axis=axis, keepdims=True)
    v = jnp.var(x, axis=axis, keepdims=True)
    return (x - m) / jnp.sqrt(v + eps)

def _scatter_add(tgt, idx, src, axis=0):
    return tgt.at[idx].add(src)

def _segment_sum(src, seg, n):
    return jax.ops.segment_sum(src, seg, n)
kernel_name = 'mk_early_fusion_d1_tok_img512_r4_7e329e'

def setup_inputs(seed: int=0):
    np.random.seed(seed)
    _w = jnp.asarray

    def _rec_inputs():
        import jax
        import jax.numpy as jnp
        _rk = jax.random.key(seed)
        x = -0.000392918 + 0.999932 * jax.random.normal(jax.random.fold_in(_rk, 1), (8, 1, 128, 128), jnp.float32)
        txt = 0.229487 + 0.681011 * jax.random.normal(jax.random.fold_in(_rk, 2), (8, 128, 128), jnp.float32)
        return (x, txt)
    x, txt = _rec_inputs()

    def _L0_tok_setup():
        import math
        import jax, jax.numpy as jnp
        import numpy as np
        PW = PH = 16
        EMB = 128
        HID = 128
        B, H, W = (64, 128, 128)
        L = H // PW * (W // PH)
        SIGMA_ZERO = 0.1

        def _f_noise(x):
            return jnp.sign(x) * jnp.sqrt(jnp.abs(x))

        def _noisy_linear(x, w, b, sw, sb, eps_in, eps_out):
            ei = _f_noise(eps_in)
            eo = _f_noise(eps_out)
            w_n = w + sw * (eo[:, None] * ei[None, :])
            b_n = b + sb * eo
            return x @ w_n.T + b_n

        def _unfold_patches(x):
            b = x.shape[0]
            p = x.reshape(b, H // PW, PW, W // PH, PH)
            p = p.transpose(0, 1, 3, 2, 4)
            return p.reshape(b, L, PW * PH)

        def _pos_encoding(x):
            pos = jnp.arange(L, dtype=jnp.float32)[:, None]
            div = jnp.exp(jnp.arange(0, EMB, 2, dtype=jnp.float32) * (-math.log(10000.0) / EMB))
            ang = pos * div
            pe = jnp.stack([jnp.sin(ang), jnp.cos(ang)], axis=-1).reshape(L, EMB)
            return x + pe[None, :, :]
        key = jax.random.key(seed)
        ks = jax.random.split(key, 12)
        in_f = PW * PH
        sig = SIGMA_ZERO / math.sqrt(in_f)
        bnd1 = 1.0 / math.sqrt(in_f)
        bnd3 = 1.0 / math.sqrt(HID)
        u = lambda k, shape, bnd: jax.random.uniform(k, shape, jnp.float32, -bnd, bnd)
        return {'inputs': jax.random.normal(ks[0], (B, 1, H, W), jnp.float32), 'W1_w': u(ks[1], (HID, in_f), bnd1), 'W1_b': u(ks[2], (HID,), bnd1), 'W1_sw': jnp.full((HID, in_f), sig, jnp.float32), 'W1_sb': jnp.full((HID,), sig, jnp.float32), 'W2_w': u(ks[3], (HID, in_f), bnd1), 'W2_b': u(ks[4], (HID,), bnd1), 'W2_sw': jnp.full((HID, in_f), sig, jnp.float32), 'W2_sb': jnp.full((HID,), sig, jnp.float32), 'W3_w': u(ks[5], (EMB, HID), bnd3), 'W3_b': u(ks[6], (EMB,), bnd3), 'eps_in1': jax.random.normal(ks[7], (in_f,), jnp.float32), 'eps_out1': jax.random.normal(ks[8], (HID,), jnp.float32), 'eps_in2': jax.random.normal(ks[9], (in_f,), jnp.float32), 'eps_out2': jax.random.normal(ks[10], (HID,), jnp.float32)}
    _L0_tok_all = _L0_tok_setup()
    _L0_tok_in = {k: v for k, v in _L0_tok_all.items() if k in ('W1_w', 'W1_b', 'W1_sw', 'W1_sb', 'W2_w', 'W2_b', 'W2_sw', 'W2_sb', 'W3_w', 'W3_b', 'eps_in1', 'eps_out1', 'eps_in2', 'eps_out2')}
    del _L0_tok_all

    def _L0_attn_setup():
        import jax, jax.numpy as jnp
        import numpy as np
        B, N, D, H = (4, 256, 128, 8)
        DH = D // H
        LAM = 0.5
        key = jax.random.key(seed)
        ks = jax.random.split(key, 7)
        s = 0.02
        return {'x': jax.random.normal(ks[0], (B, N, D), dtype=jnp.float32), 'Wq': jax.random.normal(ks[1], (D, 2 * D), dtype=jnp.float32) * s, 'bq': jax.random.normal(ks[2], (2 * D,), dtype=jnp.float32) * s, 'Wk': jax.random.normal(ks[3], (D, 2 * D), dtype=jnp.float32) * s, 'bk': jax.random.normal(ks[4], (2 * D,), dtype=jnp.float32) * s, 'Wv': jax.random.normal(ks[5], (D, D), dtype=jnp.float32) * s, 'bv': jax.random.normal(ks[6], (D,), dtype=jnp.float32) * s}
    _L0_attn_all = _L0_attn_setup()
    _L0_attn_in = {k: v for k, v in _L0_attn_all.items() if k in ('Wq', 'bq', 'Wk', 'bk', 'Wv', 'bv')}
    del _L0_attn_all

    def _L0_ffn_setup():
        import jax, jax.numpy as jnp
        import numpy as np
        E = 8
        K = 1
        D = 128
        I = 512
        B, T = (2, 512)
        key = jax.random.key(seed)
        ks = jax.random.split(key, 7)
        s = 0.02
        x = jax.random.normal(ks[0], (B, T, D), jnp.float32)
        gate_w = jax.random.normal(ks[1], (E, D), jnp.float32) * s
        w1 = jax.random.normal(ks[2], (E, I, D), jnp.float32) * s
        w2 = jax.random.normal(ks[3], (E, D, I), jnp.float32) * s
        w3 = jax.random.normal(ks[4], (E, I, D), jnp.float32) * s
        sw1 = jax.random.normal(ks[5], (I, D), jnp.float32) * s
        sw2 = jax.random.normal(ks[6], (D, I), jnp.float32) * s
        return {'x': x, 'gate_w': gate_w, 'w1': w1, 'w2': w2, 'w3': w3, 'sw1': sw1, 'sw2': sw2}
    _L0_ffn_all = _L0_ffn_setup()
    _L0_ffn_in = {k: v for k, v in _L0_ffn_all.items() if k in ('gate_w', 'w1', 'w2', 'w3', 'sw1', 'sw2')}
    del _L0_ffn_all
    return {'x': x, 'txt': txt, 'L0_tok_W1_w': _L0_tok_in['W1_w'], 'L0_tok_W1_b': _L0_tok_in['W1_b'], 'L0_tok_W1_sw': _L0_tok_in['W1_sw'], 'L0_tok_W1_sb': _L0_tok_in['W1_sb'], 'L0_tok_W2_w': _L0_tok_in['W2_w'], 'L0_tok_W2_b': _L0_tok_in['W2_b'], 'L0_tok_W2_sw': _L0_tok_in['W2_sw'], 'L0_tok_W2_sb': _L0_tok_in['W2_sb'], 'L0_tok_W3_w': _L0_tok_in['W3_w'], 'L0_tok_W3_b': _L0_tok_in['W3_b'], 'L0_tok_eps_in1': _L0_tok_in['eps_in1'], 'L0_tok_eps_out1': _L0_tok_in['eps_out1'], 'L0_tok_eps_in2': _L0_tok_in['eps_in2'], 'L0_tok_eps_out2': _L0_tok_in['eps_out2'], 'L0_attn_Wq': _L0_attn_in['Wq'], 'L0_attn_bq': _L0_attn_in['bq'], 'L0_attn_Wk': _L0_attn_in['Wk'], 'L0_attn_bk': _L0_attn_in['bk'], 'L0_attn_Wv': _L0_attn_in['Wv'], 'L0_attn_bv': _L0_attn_in['bv'], 'L0_ffn_gate_w': _L0_ffn_in['gate_w'], 'L0_ffn_w1': _L0_ffn_in['w1'], 'L0_ffn_w2': _L0_ffn_in['w2'], 'L0_ffn_w3': _L0_ffn_in['w3'], 'L0_ffn_sw1': _L0_ffn_in['sw1'], 'L0_ffn_sw2': _L0_ffn_in['sw2']}

def reference(x, txt, L0_tok_W1_w, L0_tok_W1_b, L0_tok_W1_sw, L0_tok_W1_sb, L0_tok_W2_w, L0_tok_W2_b, L0_tok_W2_sw, L0_tok_W2_sb, L0_tok_W3_w, L0_tok_W3_b, L0_tok_eps_in1, L0_tok_eps_out1, L0_tok_eps_in2, L0_tok_eps_out2, L0_attn_Wq, L0_attn_bq, L0_attn_Wk, L0_attn_bk, L0_attn_Wv, L0_attn_bv, L0_ffn_gate_w, L0_ffn_w1, L0_ffn_w2, L0_ffn_w3, L0_ffn_sw1, L0_ffn_sw2):
    import jax
    import jax.numpy as jnp

    def _L0_tok_ref(inputs, W1_w, W1_b, W1_sw, W1_sb, W2_w, W2_b, W2_sw, W2_sb, W3_w, W3_b, eps_in1, eps_out1, eps_in2, eps_out2):
        import math
        import jax, jax.numpy as jnp
        import numpy as np
        PW = PH = 16
        EMB = 128
        HID = 128
        B, H, W = (64, 128, 128)
        L = H // PW * (W // PH)
        SIGMA_ZERO = 0.1

        def _f_noise(x):
            return jnp.sign(x) * jnp.sqrt(jnp.abs(x))

        def _noisy_linear(x, w, b, sw, sb, eps_in, eps_out):
            ei = _f_noise(eps_in)
            eo = _f_noise(eps_out)
            w_n = w + sw * (eo[:, None] * ei[None, :])
            b_n = b + sb * eo
            return x @ w_n.T + b_n

        def _unfold_patches(x):
            b = x.shape[0]
            p = x.reshape(b, H // PW, PW, W // PH, PH)
            p = p.transpose(0, 1, 3, 2, 4)
            return p.reshape(b, L, PW * PH)

        def _pos_encoding(x):
            pos = jnp.arange(L, dtype=jnp.float32)[:, None]
            div = jnp.exp(jnp.arange(0, EMB, 2, dtype=jnp.float32) * (-math.log(10000.0) / EMB))
            ang = pos * div
            pe = jnp.stack([jnp.sin(ang), jnp.cos(ang)], axis=-1).reshape(L, EMB)
            return x + pe[None, :, :]
        x = _unfold_patches(inputs)
        g = _noisy_linear(x, W1_w, W1_b, W1_sw, W1_sb, eps_in1, eps_out1)
        x_gate = g * jnp.tanh(jax.nn.softplus(g))
        x_inner = _noisy_linear(x, W2_w, W2_b, W2_sw, W2_sb, eps_in2, eps_out2)
        x = x_gate * x_inner
        x = x @ W3_w.T + W3_b
        return _pos_encoding(x)

    def _L0_attn_ref(x, Wq, bq, Wk, bk, Wv, bv):
        import jax, jax.numpy as jnp
        import numpy as np
        B, N, D, H = (4, 256, 128, 8)
        DH = D // H
        LAM = 0.5
        b, n, d = x.shape
        q = (x @ Wq + bq).reshape(b, n, H, 2 * DH).transpose(0, 2, 1, 3)
        k = (x @ Wk + bk).reshape(b, n, H, 2 * DH).transpose(0, 2, 1, 3)
        v = (x @ Wv + bv).reshape(b, n, H, DH).transpose(0, 2, 1, 3)
        q1, q2 = (q[..., :DH], q[..., DH:])
        k1, k2 = (k[..., :DH], k[..., DH:])
        scale = 1.0 / jnp.sqrt(jnp.float32(DH))
        a1 = jax.nn.softmax(jnp.einsum('bhqd,bhkd->bhqk', q1, k1) * scale, axis=-1)
        a2 = jax.nn.softmax(jnp.einsum('bhqd,bhkd->bhqk', q2, k2) * scale, axis=-1)
        attn = a1 - LAM * a2
        out = jnp.einsum('bhqk,bhkd->bhqd', attn, v)
        return out.transpose(0, 2, 1, 3).reshape(b, n, d)

    def _L0_ffn_ref(x, gate_w, w1, w2, w3, sw1, sw2):
        import jax, jax.numpy as jnp
        import numpy as np
        E = 8
        K = 1
        D = 128
        I = 512
        B, T = (2, 512)
        xf = x.reshape(-1, D)
        logits = xf @ gate_w.T
        wts, idx = jax.lax.top_k(logits, K)
        wts = jax.nn.softmax(wts, axis=-1)
        comb = jnp.einsum('nke,nk->ne', jax.nn.one_hot(idx, E, dtype=xf.dtype), wts)
        h = jax.nn.silu(jnp.einsum('nd,eid->nei', xf, w1)) * jnp.einsum('nd,eid->nei', xf, w3)
        y = jnp.einsum('nei,edi->nd', h * comb[:, :, None], w2)
        y = y + jax.nn.gelu(xf @ sw1.T, approximate=False) @ sw2.T
        return y.reshape(x.shape)
    h = _L0_tok_ref(x, L0_tok_W1_w, L0_tok_W1_b, L0_tok_W1_sw, L0_tok_W1_sb, L0_tok_W2_w, L0_tok_W2_b, L0_tok_W2_sw, L0_tok_W2_sb, L0_tok_W3_w, L0_tok_W3_b, L0_tok_eps_in1, L0_tok_eps_out1, L0_tok_eps_in2, L0_tok_eps_out2)
    h = jnp.concatenate([h, txt], axis=1)
    h = h + _L0_attn_ref(_layernorm(h, axis=-1), L0_attn_Wq, L0_attn_bq, L0_attn_Wk, L0_attn_bk, L0_attn_Wv, L0_attn_bv)
    h = h + _L0_ffn_ref(_layernorm(h, axis=-1), L0_ffn_gate_w, L0_ffn_w1, L0_ffn_w2, L0_ffn_w3, L0_ffn_sw1, L0_ffn_sw2)
    return h

_drawn_inputs = setup_inputs


def setup_inputs(seed=0):
    import zlib

    import numpy as np

    out = dict(_drawn_inputs(seed))
    spreads = {'L0_tok_W1_sw': (0.0062500000931322575, 0.6),
     'L0_tok_W1_sb': (0.0062500000931322575, 0.6),
     'L0_tok_W2_sw': (0.0062500000931322575, 0.6),
     'L0_tok_W2_sb': (0.0062500000931322575, 0.6)}
    factors = {'L0_tok_W1_b': 8.0,
     'L0_tok_W2_b': 8.0,
     'L0_tok_eps_in1': 3.734,
     'L0_tok_eps_out1': 3.486,
     'L0_tok_eps_in2': 3.537,
     'L0_tok_eps_out2': 3.529,
     'L0_attn_Wq': 8.0,
     'L0_attn_bq': 8.0,
     'L0_attn_Wk': 8.0,
     'L0_attn_bk': 8.0,
     'L0_attn_bv': 3.72,
     'L0_ffn_gate_w': 3.508,
     'L0_ffn_w1': 3.446,
     'L0_ffn_w2': 3.354,
     'L0_ffn_w3': 3.316}
    for name, (base, spread) in spreads.items():
        noise = np.random.default_rng([zlib.crc32(name.encode()), seed]).standard_normal(out[name].shape)
        drawn = base * np.exp(spread * noise) if base else spread * noise
        out[name] = jnp.asarray(drawn.astype(out[name].dtype))
    for name, factor in factors.items():
        out[name] = (out[name] * factor).astype(out[name].dtype)
    return out
```

```python
import math

import numpy as np

import concourse.bass as bass
from concourse import mybir
from contextlib import ExitStack

B, IMG_SIDE, PATCH = 8, 128, 16
SIDE = IMG_SIDE // PATCH
N_IMG, N_TXT = SIDE * SIDE, 128
SEQ = N_IMG + N_TXT
D = 128
T = B * SEQ // 128
PAIRS = B // 2
TJ = 3
PT = TJ * 128
HEADS, DH = 8, 16
HS = 2 * HEADS
HSC = 8
LAM = 0.5
KC = PATCH * PATCH // 128
E, I = 8, 512
IC = I // 128
SLOT_TILES = (B * SEQ + E * 127) // 128
EPS = 1e-5
NPART = 3
K_PARTS = (0, 1, 2, 0, 1, 0)
Q_PARTS = (0, 0, 0, 1, 1, 2)
SROWS = 16 * len(K_PARTS)
SHALF = SEQ - 128

W_COLS = dict(wq=2 * D, wk=2 * D, wv=D, w3=D, sw1=I, sw2=IC * D, gate=E)
C_COLS = dict(ident=128, tri=128, ones=128, pe=128, tile_no=SLOT_TILES, prio=E)
N_COLS = dict(ei1=KC, ei2=KC, eo1=1, eo2=1, b1=1, sb1=1, b2=1, sb2=1, bq=2, bk=2)


def columns(cols):
    at, out = 0, {}
    for name, n in cols.items():
        out[name] = slice(at, at + n)
        at += n
    return out, at


def build_kernel(nc, xT, txt, wn, npack, rows, wpack, cpack, w13, w2, out):
    F32, BF16 = mybir.dt.float32, mybir.dt.bfloat16
    I32, U32 = mybir.dt.int32, mybir.dt.uint32
    ALU, ACT, AX = mybir.AluOpType, mybir.ActivationFunctionType, mybir.AxisListType
    WC, WN = columns(W_COLS)
    CC, CN = columns(C_COLS)
    NC_, NN = columns(N_COLS)

    split_dram = nc.dram_tensor("split_scratch", [4 * PAIRS, NPART, 128, PT], BF16, kind="Internal").ap()
    xs_dram = nc.dram_tensor("xs_scratch", [SLOT_TILES * 128, D], F32, kind="Internal").ap()
    ys_dram = nc.dram_tensor("ys_scratch", [SLOT_TILES * 128, D], F32, kind="Internal").ap()

    ctx = ExitStack()
    with ctx:
        def sb(name, shape, dt=F32):
            return ctx.enter_context(nc.sbuf_tensor(name, shape, dt))

        def sem(name):
            return ctx.enter_context(nc.semaphore(name))

        bank = [ctx.enter_context(nc.psum_tensor(f"bank{i}", [128, 512], F32)) for i in range(8)]

        NST = 3
        stacks = sb("stacks", [128, 2 * NST, HS * PT], BF16)
        free_q = stacks[:, NST - 1, :].bitcast(F32)
        free_k = stacks[:, 2 * NST - 1, :].bitcast(F32)
        x_sb = free_k[:, 0:1024].rearrange("p (c t) -> p c t", c=KC)
        wn_sb = free_k[:, 1024:2048].rearrange("p (m c n) -> p m c n", m=4, c=KC)
        np_sb = sb("np_sb", [128, NN])
        rows_sb = sb("rows_sb", [128, 4, 128])
        wp_sb = sb("wp_sb", [128, WN])
        c_sb = sb("c_sb", [128, CN])
        w13_sb = sb("w13_sb", [128, E, 2, I])
        w2_sb = sb("w2_sb", [128, E, IC, D])

        def W(name):
            return wp_sb[:, WC[name]]

        def C(name):
            return c_sb[:, CC[name]]

        def N(name):
            return np_sb[:, NC_[name]]

        ident = C("ident")

        noise = sb("noise", [128, 262])
        hn = sb("hn", [128, T, D])
        nz_abs, nz_y, nz_u = [hn[:, :, :].rearrange("p t d -> p (t d)")[:, 262 * i:262 * (i + 1)] for i in range(3)]
        wt = free_k[:, 2048:2304].rearrange("p (c n) -> p c n", c=KC)
        w1n = free_k[:, 2304:2560].rearrange("p (c n) -> p c n", c=KC)
        w2n = free_k[:, 2560:2816].rearrange("p (c n) -> p c n", c=KC)
        bn_ = sb("bn_", [128, 2])
        bq4 = sb("bq4", [128, 2])
        peb = sb("peb", [128, 128])
        g_sb = free_q[:, 0:512]
        inner = free_q[:, 512:1024]
        gm = free_q[:, 1024:1536]
        ex = free_q[:, 1536:2048]
        mu = free_q[:, 2048:2560]
        mr = free_q[:, 2560:3072]

        h = sb("h", [128, T, D])
        hnT = sb("hnT", [128, T * 128])
        stats = sb("stats", [128, T, 6])
        mv = sb("mv", [128, T, 2])
        ve = sb("ve", [128, T])
        rstd = sb("rstd", [128, T])
        ln_u = sb("ln_u", [128, T])

        NF = 4
        f_ring = sb("f_ring", [128, NF, PT])
        r1 = sb("r1", [128, PT])
        parts = sb("parts", [128, NF, NPART, PT], BF16)
        q_st, k_st = [[stacks[:, NST * m + i, :].rearrange("p (g t) -> p g t", g=HS) for i in range(NST)] for m in range(2)]
        vaug = sb("vaug", [128, T, HEADS, 32])
        smax = sb("smax", [128, 2, TJ, HS])
        mx_f = sb("mx_f", [HS, PT])
        mx_r = sb("mx_r", [HS, PT])
        mx_p = sb("mx_p", [HS, NPART, PT], BF16)
        NPT = 6
        p_ring = sb("p_ring", [128, NPT, 2, SEQ])
        oT = sb("oT", [128, 2, 2, PT])
        rs = sb("rs", [128, HS])
        o1 = sb("o1", [128, HS, DH])
        o2 = sb("o2", [128, D])

        lg = sb("lg", [128, T, E])
        mxl = sb("mxl", [128, T])
        oh = sb("oh", [128, T, E])
        oh_b = sb("oh_b", [128, T, E], BF16)
        tri_b = sb("tri_b", [128, 128], BF16)
        ones_b = sb("ones_b", [128, 128], BF16)
        cnt = sb("cnt", [128, E])
        cnt_i = sb("cnt_i", [128, E], I32)
        tiles_e = sb("tiles_e", [128, E])
        incl = sb("incl", [128, E])
        base = sb("base", [128, E])
        one8 = sb("one8", [128, E])
        slot_f = sb("slot_f", [128, T])
        slot_u = sb("slot_u", [128, T], U32)
        cmp = sb("cmp", [128, SLOT_TILES, E])
        et_f = sb("et_f", [128, SLOT_TILES])
        et_i = sb("et_i", [128, SLOT_TILES], I32)
        zero = sb("zero", [128, SLOT_TILES * D // 8])
        spare = stacks[:, :, :].rearrange("p a x -> p (a x)").bitcast(F32)
        at = [0]

        def carve(*shape):
            n = math.prod(shape)
            at[0] += n
            v = spare[:, at[0] - n:at[0]]
            if len(shape) == 1:
                return v
            names = "abc"[:len(shape)]
            return v.rearrange(f"p ({' '.join(names)}) -> p {' '.join(names)}", **dict(zip(names, shape)))

        a_sh = carve(2, IC, 512)
        NX = 3
        xs = carve(NX, D)
        xsT = carve(2, D)
        sA = carve(2, I)
        gate_sb = carve(2, I)
        gT = carve(2, I)
        NY = 3
        y_sb = carve(NY, D)
        yg = carve(T, D)

        ld_x, ld_wn, ld_rows, ld_wp, ld_c, ld_txt, ld_np = [sem(f"ld_{n}") for n in ("x", "wn", "rows", "wp", "c", "txt", "np")]
        ld_exp = sem("ld_exp")
        dve_step, pool_step, act_step = sem("dve_step"), sem("pool_step"), sem("act_step")
        noisy = sem("noisy")
        tok_mm = sem("tok_mm")
        g_done = sem("g_done")
        gm_done = sem("gm_done")
        ex_done = sem("ex_done")
        act_done = sem("act_done")
        h_mm = sem("h_mm")
        hn_ready = sem("hn_ready")
        tr_done = sem("tr_done")
        hnT_done = sem("hnT_done")
        bq_done = sem("bq_done")
        misc_ready = sem("misc_ready")
        out_read = sem("out_read")
        f_done = sem("f_done")
        hi_done = sem("hi_done")
        split_done = sem("split_done")
        split_wr = [sem(f"split_wr{i}") for i in range(NF)]
        stack_ld = [sem(f"stack_ld{i}") for i in range(NST)]
        max_ld = [sem(f"max_ld{i}") for i in range(NST)]
        init_done = sem("init_done")
        ones_done = sem("ones_done")
        v_done = sem("v_done")
        s_ready, s_max = sem("s_ready"), sem("s_max")
        mx_evac, mx_hi, mx_split = sem("mx_evac"), sem("mx_hi"), sem("mx_split")
        st_ready, exp_done = sem("st_ready"), sem("exp_done")
        av_done, av_free = sem("av_done"), sem("av_free")
        h2_done = sem("h2_done")
        lg_mm, oh_done, rank_mm, slot_done, et_done = [sem(n) for n in ("lg_mm", "oh_done", "rank_mm", "slot_done", "et_done")]
        zero_done, xs_zeroed, scattered = sem("zero_done"), sem("xs_zeroed"), sem("scattered")
        sh_mm, sh_act, sh_y, sh_add = [sem(n) for n in ("sh_mm", "sh_act", "sh_y", "sh_add")]
        xs_ld = [sem(f"xs_ld{i}") for i in range(NX)]
        x_tr, x_cp, up_a, up_b, silu_done, gated, g_tr, g_cp, y_mm, y_cp = [sem(n) for n in (
            "x_tr", "x_cp", "up_a", "up_b", "silu_done", "gated", "g_tr", "g_cp", "y_mm", "y_cp")]
        ys_st = [sem(f"ys_st{i}") for i in range(NY)]
        gath = [sem(f"gath{i}") for i in range(T)]
        fin_add = sem("fin_add")
        stored = sem("stored")

        def proj_items(p):
            return [("proj", p, n) for n in range(5)]

        misc_order = proj_items(0) + proj_items(1) + [("max", 0, 0)]
        for p in range(PAIRS):
            if p + 2 < PAIRS:
                misc_order += proj_items(p + 2)
            if p + 1 < PAIRS:
                misc_order += [("max", p + 1, 0)]
            misc_order += [("out", p, j) for j in range(TJ)]
        misc_no = {item: n for n, item in enumerate(misc_order)}

        def mbank(item):
            return bank[6 + misc_no[item] % 2]

        def evacuated(item):
            kind, p, n = item
            if kind == "proj":
                return (f_done, 4 * p + n + 1) if n < 4 else (v_done, p + 1)
            return (mx_evac, p + 1) if kind == "max" else (out_read, TJ * p + n + 1)

        def batches(j):
            return {0: [(0, 128, 0)], 1: [(0, SHALF, 0), (SHALF, 128 - SHALF, 1)], 2: [(0, 128, 1)]}[j]

        block = ctx.enter_context(nc.Block())

        @block.sync
        def _(sp):
            sp.dma_start(wn_sb[:, :, :, :], wn).then_inc(ld_wn, 16)
            sp.dma_start(rows_sb[:, :, :], rows.to_broadcast([128, 4, 128])).then_inc(ld_rows, 16)
            sp.dma_start(np_sb[:, :], npack).then_inc(ld_np, 16)
            sp.dma_start(x_sb[:, :, :], xT).then_inc(ld_x, 16)
            sp.dma_start(c_sb[:, :], cpack).then_inc(ld_c, 16)
            for b in range(B):
                p, odd = divmod(b, 2)
                if odd:
                    sp.dma_start(h[:, TJ * p + 2, :], txt[b, :, :]).then_inc(ld_txt, 16)
                else:
                    sp.dma_start(h[N_IMG:128, TJ * p, :], txt[b, 0:128 - N_IMG, :]).then_inc(ld_txt, 16)
                    sp.dma_start(h[0:SHALF, TJ * p + 1, :], txt[b, 128 - N_IMG:128, :]).then_inc(ld_txt, 16)
            sp.dma_start(wp_sb[:, :], wpack).then_inc(ld_wp, 16)

            def store_parts(r):
                sp.wait_ge(split_done, r + 1)
                sp.dma_start(split_dram[r, :, :, :].rearrange("s x t -> x s t"), parts[:, r % NF, :, :])\
                    .then_inc(split_wr[r % NF], 16)

            def load_stacks(p):
                b = p % NST
                if p >= NST:
                    sp.wait_ge(st_ready, TJ * HEADS * (p - NST + 1))
                for n in range(4):
                    r = 4 * p + n
                    st, order = (q_st[b], Q_PARTS) if n < 2 else (k_st[b], K_PARTS)
                    sp.wait_ge(split_wr[r % NF], 16 * (r // NF + 1))
                    src = split_dram[r, :, :, :].rearrange("s (d g) t -> (s d) (g t)", g=HSC)
                    ch = n % 2
                    if n < 2:
                        blocks = [(j, 1, s) for j, s in enumerate(order)]
                    else:
                        blocks = [(0, 3, 0), (3, 2, 0), (5, 1, 0)]
                    for j, m, s in blocks:
                        sp.dma_start(st[16 * j:16 * (j + m), HSC * ch:HSC * (ch + 1), :].rearrange("p g t -> p (g t)"),
                                     src[16 * s:16 * (s + m), :]).then_inc(stack_ld[b], 16)

            def load_max(p):
                b = p % NST
                sp.wait_ge(mx_split, p + 1)
                for s in range(NPART):
                    sp.dma_start(q_st[b][SROWS + s:SROWS + s + 1, :, :], mx_p[:, s, :]).then_inc(max_ld[b], 16)

            def load_experts(p):
                n = E // PAIRS
                for e in range(p * n, (p + 1) * n):
                    sp.dma_start(w13_sb[:, e, :, :], w13[e, :, :, :]).then_inc(ld_exp, 16)
                    sp.dma_start(w2_sb[:, e, :, :], w2[e, :, :, :]).then_inc(ld_exp, 16)

            for p in range(2):
                for n in range(4):
                    store_parts(4 * p + n)
                load_stacks(p)
            sp.wait_ge(zero_done, 1)
            for i in range(8):
                c = SLOT_TILES * D // 8
                sp.dma_start(xs_dram.rearrange("(p r) d -> p (r d)", p=128)[:, c * i:c * (i + 1)], zero[:, :]).then_inc(xs_zeroed, 16)
            load_experts(0)
            load_max(0)
            for p in range(PAIRS):
                if p + 2 < PAIRS:
                    for n in range(4):
                        store_parts(4 * (p + 2) + n)
                    load_stacks(p + 2)
                if p + 1 < PAIRS:
                    load_experts(p + 1)
                    load_max(p + 1)

            sp.wait_ge(scattered, 16 * T)
            def load_xs(t):
                if t >= NX:
                    sp.wait_ge(x_tr, t - NX + 1)
                sp.dma_start(xs[:, t % NX, :], xs_dram[128 * t:128 * (t + 1), :]).then_inc(xs_ld[t % NX], 16)
            def store_ys(t):
                sp.wait_ge(y_cp, t + 1)
                sp.dma_start(ys_dram[128 * t:128 * (t + 1), :], y_sb[:, t % NY, :]).then_inc(ys_st[t % NY], 16)
            for t in range(NX):
                load_xs(t)
            for t in range(SLOT_TILES):
                if t + NX < SLOT_TILES:
                    load_xs(t + NX)
                store_ys(t)
            for t in range(T):
                sp.wait_ge(fin_add, t + 1)
                sp.dma_start(out[128 * t:128 * (t + 1), :], yg[:, t, :]).then_inc(stored, 16)
            sp.wait_ge(stored, 16 * T)

        @block.gpsimd
        def _(pool):
            steps = [0]

            def link(ins):
                steps[0] += 1
                ins.then_inc(pool_step, 1)
                pool.wait_ge(pool_step, steps[0])

            pool.memset(zero[:, :], 0.0).then_inc(zero_done, 1)
            pool.wait_ge(zero_done, 1)
            for b in range(NST):
                if b == NST - 1:
                    pool.wait_ge(h_mm, 1)
                pool.memset(k_st[b][SROWS:SROWS + NPART, :, :], 1.0).then_inc(ones_done, 1)
                pool.wait_ge(ones_done, b + 1)

            def split(r):
                pool.wait_ge(f_done, r + 1)
                pool.wait_ge(hi_done, r + 1)
                f, pr = f_ring[:, r % NF, :], parts[:, r % NF, :, :]
                link(pool.tensor_tensor(r1[:, :], f, pr[:, 0, :], ALU.subtract))
                link(pool.tensor_scalar(pr[:, 1, :], r1[:, :], 1.0, 0.0, ALU.mult, ALU.add))
                pool.tensor_tensor(pr[:, 2, :], r1[:, :], pr[:, 1, :], ALU.subtract).then_inc(split_done, 1)
                pool.wait_ge(split_done, r + 1)

            def split_max(p):
                pool.wait_ge(mx_evac, p + 1)
                pool.wait_ge(mx_hi, p + 1)
                link(pool.tensor_tensor(mx_r[:, :], mx_f[:, :], mx_p[:, 0, :], ALU.subtract))
                link(pool.tensor_scalar(mx_p[:, 1, :], mx_r[:, :], 1.0, 0.0, ALU.mult, ALU.add))
                pool.tensor_tensor(mx_p[:, 2, :], mx_r[:, :], mx_p[:, 1, :], ALU.subtract).then_inc(mx_split, 1)
                pool.wait_ge(mx_split, p + 1)

            for r in range(8):
                split(r)
            split_max(0)
            for p in range(PAIRS):
                if p + 2 < PAIRS:
                    for n in range(4):
                        split(4 * (p + 2) + n)
                if p + 1 < PAIRS:
                    split_max(p + 1)

            pool.wait_ge(slot_done, 1)
            pool.wait_ge(xs_zeroed, 16 * 8)
            for t in range(T):
                pool.indirect_dma_start(out=xs_dram, out_offset=bass.IndirectOffsetOnAxis(ap=slot_u[:, t:t + 1], axis=0),
                                        in_=hn[:, t, :], in_offset=None).then_inc(scattered, 16)
            for i in range(NY):
                pool.wait_ge(ys_st[i], 16 * len(range(i, SLOT_TILES, NY)))
            for t in range(T):
                pool.indirect_dma_start(out=yg[:, t, :], out_offset=None, in_=ys_dram,
                                        in_offset=bass.IndirectOffsetOnAxis(ap=slot_u[:, t:t + 1], axis=0)).then_inc(gath[t], 16)

        @block.scalar
        def _(act):
            act.wait_ge(tok_mm, 1)
            act.wait_ge(noisy, 3)
            act.activation(g_sb[:, :], bank[0][:, :], ACT.Identity, bias=bn_[:, 0:1]).then_inc(g_done, 1)
            act.wait_ge(gm_done, 1)
            act.activation(ex[:, :], gm[:, :], ACT.Exp).then_inc(ex_done, 1)

            def copy_hnT(n):
                act.wait_ge(tr_done, n + 1)
                c = 512 * (n % 3)
                act.activation(hnT[:, c:c + 512], bank[n % 3][:, :], ACT.Copy).then_inc(hnT_done, 1)

            for n in range(3):
                copy_hnT(n)
            act.wait_ge(bq_done, 1)

            def evac_proj(p):
                for n in range(4):
                    r = 4 * p + n
                    item = ("proj", p, n)
                    act.wait_ge(misc_ready, misc_no[item] + 1)
                    if r >= NF:
                        act.wait_ge(split_done, r - NF + 1)
                    bias = bq4[:, n:n + 1] if n < 2 else N("bk")[:, n - 2:n - 1]
                    act.activation(f_ring[:, r % NF, :], mbank(item)[:, 0:PT], ACT.Identity, bias=bias,
                                   scale=DH ** -0.5 if n < 2 else 1.0).then_inc(f_done, 1)

            def evac_max(p):
                item = ("max", p, 0)
                act.wait_ge(misc_ready, misc_no[item] + 1)
                if p >= 1:
                    act.wait_ge(max_ld[(p - 1) % NST], 16 * NPART * ((p - 1) // NST + 1))
                act.activation(mx_f[:, :], mbank(item)[0:HS, 0:PT], ACT.Copy).then_inc(mx_evac, 1)
                act.wait_ge(mx_evac, p + 1)
                act.activation(mx_p[:, 0, :], mx_f[:, :], ACT.Copy).then_inc(mx_hi, 1)

            def exp(p, hd, j):
                g = TJ * (HEADS * p + hd) + j
                act.wait_ge(st_ready, g + 1)
                if g >= NPT:
                    act.wait_ge(av_done, (g - NPT) // TJ + 1)
                act.activation(p_ring[:, g % NPT, :, :], bank[2 + g % 2][:, 0:2 * SEQ].rearrange("p (s q) -> p s q", s=2),
                               ACT.Exp).then_inc(exp_done, 1)

            def evac_av(p, hg):
                act.wait_ge(av_done, HEADS * p + 4 * (hg + 1))
                if p >= 1 and hg == 0:
                    act.wait_ge(misc_ready, misc_no[("out", p - 1, TJ - 1)] + 1)
                for bb in range(2):
                    act.activation(oT[:, hg, :, SEQ * bb:SEQ * (bb + 1)],
                                   bank[4 + bb][:, 0:2 * SEQ].rearrange("p (s q) -> p s q", s=2), ACT.Copy).then_inc(av_free, 1)

            evac_proj(0)
            evac_proj(1)
            evac_max(0)
            for p in range(PAIRS):
                for hd in range(HEADS):
                    for j in range(TJ):
                        exp(p, hd, j)
                        if hd == 4 and j == 1:
                            evac_av(p, 0)
                    if hd == 2 and p + 2 < PAIRS:
                        evac_proj(p + 2)
                    if hd == 6 and p + 1 < PAIRS:
                        evac_max(p + 1)
                evac_av(p, 1)

            for n in range(3, 6):
                copy_hnT(n)
            for k in range(3 * IC):
                act.wait_ge(sh_mm, k + 1)
                tc, ic = divmod(k, IC)
                if tc >= 2:
                    act.wait_ge(sh_y, tc - 1)
                act.activation(a_sh[:, tc % 2, ic, :], bank[k % 4][:, :], ACT.Gelu).then_inc(sh_act, 1)

            def silu(t):
                act.wait_ge(up_a, t + 1)
                if t >= 2:
                    act.wait_ge(gated, t - 1)
                act.activation(sA[:, t % 2, :], bank[t % 2][:, :], ACT.Silu).then_inc(silu_done, 1)

            def copy_gT(t):
                act.wait_ge(g_tr, t + 1)
                if t >= 2:
                    act.wait_ge(y_mm, t - 1)
                act.activation(gT[:, t % 2, :], bank[4][:, :], ACT.Copy).then_inc(g_cp, 1)

            for t in range(SLOT_TILES):
                silu(t)
                if t >= 1:
                    copy_gT(t - 1)
            copy_gT(SLOT_TILES - 1)

        @block.vector
        def _(dve):
            steps = [0]

            def link(ins):
                steps[0] += 1
                ins.then_inc(dve_step, 1)
                dve.wait_ge(dve_step, steps[0])

            def rsqrt(y, v, u):
                vi, yi = v.bitcast(U32), y.bitcast(I32)
                link(dve.tensor_scalar(y.bitcast(U32), vi, 1, None, ALU.logical_shift_right))
                link(dve.tensor_scalar(yi, yi, -1.0, float(0x5F3759DF), ALU.mult, ALU.add))
                for _ in range(3):
                    link(dve.tensor_tensor(u, v, y, ALU.mult))
                    link(dve.scalar_tensor_tensor(u, u, -0.5, y, ALU.mult, ALU.mult))
                    link(dve.scalar_tensor_tensor(y, u, 1.5, y, ALU.add, ALU.mult))

            dve.wait_ge(ld_rows, 16)
            dve.wait_ge(ld_np, 16)
            dve.tensor_copy(noise[:, 0:256], rows_sb[:, 0:2, :].rearrange("p a b -> p (a b)")).then_inc(dve_step, 1)
            steps[0] += 1
            link(dve.tensor_copy(noise[:, 256:262], np_sb[:, 0:6]))
            link(dve.tensor_scalar(nz_abs.bitcast(U32), noise[:, :].bitcast(U32), 0x7FFFFFFF, None, ALU.bitwise_and))
            rsqrt(nz_y, nz_abs, nz_u)
            link(dve.tensor_tensor(noise[:, :], noise[:, :], nz_y, ALU.mult))
            dve.wait_ge(ld_wn, 16)
            for m, wdst in enumerate((w1n, w2n)):
                eo = noise[:, 128 * m:128 * (m + 1)]
                for kc in range(KC):
                    ei = noise[:, 256 + 2 * m + kc:257 + 2 * m + kc]
                    link(dve.scalar_tensor_tensor(wt[:, kc, :], eo, ei, wn_sb[:, 2 * m + 1, kc, :], ALU.mult, ALU.mult))
                    ins = dve.tensor_tensor(wdst[:, kc, :], wt[:, kc, :], wn_sb[:, 2 * m, kc, :], ALU.add)
                ins.then_inc(noisy, 1)
            for m, (bb, ss) in enumerate((("b1", "sb1"), ("b2", "sb2"))):
                ins = dve.scalar_tensor_tensor(bn_[:, m:m + 1], N(ss), noise[:, 260 + m:261 + m], N(bb), ALU.mult, ALU.add)
            ins.then_inc(noisy, 1)
            dve.tensor_scalar(bq4[:, :], N("bq"), DH ** -0.5, None, ALU.mult).then_inc(bq_done, 1)
            dve.wait_ge(ld_c, 16)
            link(dve.tensor_tensor(peb[:, :], C("pe"), rows_sb[:, 2, :], ALU.add))
            dve.tensor_copy(tri_b[:, :], C("tri"))
            dve.tensor_copy(ones_b[:, :], C("ones"))
            dve.memset(one8[:, :], 1.0)
            dve.memset(vaug[:, :, :, DH:DH + 1], 1.0)
            dve.memset(vaug[:, :, :, DH + 1:32], 0.0).then_inc(init_done, 1)

            dve.wait_ge(g_done, 1)
            dve.wait_ge(noisy, 3)
            dve.tensor_scalar(gm[:, :], g_sb[:, :], 20.0, None, ALU.min).then_inc(gm_done, 1)
            dve.wait_ge(tok_mm, 2)
            link(dve.tensor_scalar(inner[:, :], bank[1][:, :], bn_[:, 1:2], None, ALU.add))
            link(dve.tensor_tensor(inner[:, :], inner[:, :], g_sb[:, :], ALU.mult))
            dve.wait_ge(ex_done, 1)
            link(dve.scalar_tensor_tensor(mu[:, :], ex[:, :], 2.0, ex[:, :], ALU.add, ALU.mult))
            link(dve.tensor_scalar(mr[:, :], mu[:, :], 2.0, None, ALU.add))
            link(dve.reciprocal(ex[:, :], mr[:, :]))
            link(dve.tensor_tensor(mu[:, :], mu[:, :], ex[:, :], ALU.mult))
            dve.tensor_tensor(g_sb[:, :], mu[:, :], inner[:, :], ALU.mult).then_inc(act_done, 1)

            dve.wait_ge(h_mm, 1)
            hv = h[:, :, :].rearrange("p (a j) d -> p a j d", j=TJ)
            for odd in range(2):
                q = slice(64 * odd, 64 * odd + 64)
                pb = peb[q, :].rearrange("p (a d) -> p a d", a=1).to_broadcast([64, PAIRS, D])
                link(dve.tensor_tensor(hv[q, :, odd, :], bank[2][q, :].rearrange("p (a d) -> p a d", a=PAIRS), pb, ALU.add))
            dve.wait_ge(ld_txt, 16 * 3 * PAIRS)

            def layer_norm():
                for t in range(T):
                    ins = dve.bn_stats(stats[:, t, :], h[:, t, :])
                link(ins)
                for t in range(T):
                    ins = dve.bn_aggr(mv[:, t, :], stats[:, t, :])
                link(ins)
                link(dve.tensor_scalar(ve[:, :], mv[:, :, 1], EPS, None, ALU.add))
                rsqrt(rstd[:, :], ve[:, :], ln_u[:, :])
                for t in range(T):
                    dve.tensor_scalar(hn[:, t, :], h[:, t, :], mv[:, t, 0:1], rstd[:, t:t + 1], ALU.subtract, ALU.mult)\
                        .then_inc(hn_ready, 1)

            layer_norm()

            def high_part(p):
                for n in range(4):
                    r = 4 * p + n
                    dve.wait_ge(f_done, r + 1)
                    if r >= NF:
                        dve.wait_ge(split_wr[r % NF], 16 * (r // NF))
                    dve.tensor_copy(parts[:, r % NF, 0, :], f_ring[:, r % NF, :]).then_inc(hi_done, 1)
                item = ("proj", p, 4)
                dve.wait_ge(misc_ready, misc_no[item] + 1)
                bv = rows_sb[:, 3:4, :].rearrange("p a (h d) -> p a h d", d=DH).to_broadcast([128, TJ, HEADS, DH])
                for j in range(TJ):
                    ins = dve.tensor_tensor(vaug[:, TJ * p + j, :, 0:DH], mbank(item)[:, 128 * j:128 * (j + 1)].rearrange("p (h d) -> p h d", d=DH),
                                            bv[:, j, :, :], ALU.add)
                ins.then_inc(v_done, 1)

            def row_max(p, hd, j):
                g = TJ * (HEADS * p + hd) + j
                dve.wait_ge(s_ready, g + 1)
                if p >= 2 and g % (TJ * HEADS) == 0:
                    dve.wait_ge(misc_ready, misc_no[("max", p - 2, 0)] + 1)
                dve.tensor_reduce(smax[:, p % 2, j, 2 * hd:2 * hd + 2], bank[g % 2][:, 0:2 * SEQ].rearrange("p (s k) -> p s k", s=2),
                                  AX.X, ALU.max, negate=True).then_inc(s_max, 1)

            def attn_out(p):
                for j in range(TJ):
                    item = ("out", p, j)
                    dve.wait_ge(misc_ready, misc_no[item] + 1)
                    v = mbank(item)[:, :].rearrange("p (a c) -> p a c", c=32)
                    link(dve.reciprocal(rs[:, :], v[:, :, DH]))
                    rv = rs[:, :].rearrange("p (a s b) -> p a s b", s=2, b=4)
                    link(dve.tensor_scalar(rv[:, :, 1, :], rv[:, :, 1, :], -LAM, None, ALU.mult))
                    ins = dve.tensor_tensor(o1[:, :, :], v[:, :, 0:DH], rs[:, :].rearrange("p (a c) -> p a c", c=1).to_broadcast([128, HS, DH]), ALU.mult)
                    ins.then_inc(out_read, 1)
                    dve.wait_ge(out_read, TJ * p + j + 1)
                    ov = o1[:, :, :].rearrange("p (a s b) d -> p a s (b d)", s=2, b=4)
                    link(dve.tensor_tensor(o2[:, :].rearrange("p (a x) -> p a x", a=2), ov[:, :, 0, :], ov[:, :, 1, :], ALU.add))
                    link(dve.tensor_tensor(h[:, TJ * p + j, :], h[:, TJ * p + j, :], o2[:, :], ALU.add))

            high_part(0)
            high_part(1)
            for hd in range(HEADS):
                for j in range(TJ):
                    row_max(0, hd, j)
            for p in range(PAIRS):
                nxt = [(p + 1, a // TJ, a % TJ) for a in range(TJ * HEADS)] if p + 1 < PAIRS else []
                for hd in range(HEADS):
                    for g in nxt[4 * hd:4 * hd + 4]:
                        row_max(*g)
                    if hd == 2 and p + 2 < PAIRS:
                        high_part(p + 2)
                attn_out(p)

            layer_norm()

            dve.wait_ge(lg_mm, 1)
            link(dve.tensor_copy(lg[:, :, :], bank[7][:, 0:T * E].rearrange("p (t e) -> p t e", e=E)))
            link(dve.tensor_reduce(mxl[:, :], lg[:, :, :], AX.X, ALU.max))
            def wide(ap):
                return ap.rearrange("p (t a) -> p t a", a=1).to_broadcast([128, T, E])
            def over_tiles(ap):
                return ap.rearrange("p (a e) -> p a e", a=1).to_broadcast([128, T, E])
            link(dve.tensor_tensor(oh[:, :, :], lg[:, :, :], wide(mxl[:, :]), ALU.is_ge))
            link(dve.tensor_tensor(oh[:, :, :], oh[:, :, :], over_tiles(C("prio")), ALU.mult))
            link(dve.tensor_reduce(mxl[:, :], oh[:, :, :], AX.X, ALU.max))
            link(dve.tensor_tensor(oh[:, :, :], oh[:, :, :], wide(mxl[:, :]), ALU.is_equal))
            dve.tensor_copy(oh_b[:, :, :], oh[:, :, :]).then_inc(oh_done, 1)
            dve.wait_ge(rank_mm, 1)
            link(dve.tensor_scalar(cnt[:, :], bank[7][:, 128:128 + E], 127.0, None, ALU.add))
            link(dve.tensor_copy(cnt_i[:, :], cnt[:, :]))
            link(dve.tensor_scalar(cnt_i[:, :], cnt_i[:, :], 7, None, ALU.arith_shift_right))
            link(dve.tensor_copy(tiles_e[:, :], cnt_i[:, :]))
            link(dve.tensor_tensor_scan(incl[:, :], one8[:, :], tiles_e[:, :], 0.0, ALU.mult, ALU.add))
            link(dve.tensor_tensor(base[:, :], incl[:, :], tiles_e[:, :], ALU.subtract))
            link(dve.tensor_scalar(base[:, :], base[:, :], 128.0, None, ALU.mult))
            link(dve.tensor_tensor(lg[:, :, :], bank[7][:, 0:T * E].rearrange("p (t e) -> p t e", e=E), over_tiles(base[:, :]), ALU.add))
            link(dve.tensor_tensor(lg[:, :, :], lg[:, :, :], oh[:, :, :], ALU.mult))
            link(dve.tensor_reduce(slot_f[:, :], lg[:, :, :], AX.X, ALU.add))
            dve.tensor_copy(slot_u[:, :], slot_f[:, :]).then_inc(slot_done, 1)
            link(dve.tensor_tensor(cmp[:, :, :], incl[:, :].rearrange("p (a e) -> p a e", a=1).to_broadcast([128, SLOT_TILES, E]),
                                   C("tile_no").rearrange("p (t a) -> p t a", a=1).to_broadcast([128, SLOT_TILES, E]), ALU.is_le))
            link(dve.tensor_reduce(et_f[:, :], cmp[:, :, :], AX.X, ALU.add))
            link(dve.tensor_scalar(et_f[:, :], et_f[:, :], E - 1.0, None, ALU.min))
            dve.tensor_copy(et_i[:, :], et_f[:, :]).then_inc(et_done, 1)

            for tc in range(3):
                dve.wait_ge(sh_y, tc + 1)
                hv4 = h[:, 4 * tc:4 * tc + 4, :].rearrange("p t d -> p (t d)")
                dve.tensor_tensor(hv4, bank[4 + tc % 2][:, :], hv4, ALU.add).then_inc(sh_add, 1)

            def copy_x(t):
                dve.wait_ge(x_tr, t + 1)
                if t >= 2:
                    dve.wait_ge(up_b, t - 1)
                dve.tensor_copy(xsT[:, t % 2, :], bank[5][:, 0:D]).then_inc(x_cp, 1)

            def gate(t):
                dve.wait_ge(up_b, t + 1)
                dve.wait_ge(silu_done, t + 1)
                if t >= 2:
                    dve.wait_ge(g_tr, t - 1)
                dve.tensor_tensor(gate_sb[:, t % 2, :], bank[2 + t % 2][:, :], sA[:, t % 2, :], ALU.mult).then_inc(gated, 1)

            def copy_y(t):
                dve.wait_ge(y_mm, t + 1)
                if t >= NY:
                    dve.wait_ge(ys_st[t % NY], 16 * (t // NY))
                dve.tensor_copy(y_sb[:, t % NY, :], bank[6 + t % 2][:, 0:D]).then_inc(y_cp, 1)

            copy_x(0)
            for t in range(SLOT_TILES):
                gate(t)
                if t >= 1:
                    copy_y(t - 1)
                if t + 1 < SLOT_TILES:
                    copy_x(t + 1)
            copy_y(SLOT_TILES - 1)
            for t in range(T):
                dve.wait_ge(gath[t], 16)
                dve.wait_ge(sh_add, 3)
                dve.tensor_tensor(yg[:, t, :], yg[:, t, :], h[:, t, :], ALU.add).then_inc(fin_add, 1)

        @block.tensor
        def _(pe):
            pe.wait_ge(ld_x, 16)
            for m, wsrc in enumerate((w1n, w2n)):
                pe.wait_ge(noisy, m + 1)
                for kc in range(KC):
                    ins = pe.matmul(bank[m][:, :], wsrc[:, kc, :], x_sb[:, kc, :], start=(kc == 0), stop=(kc == KC - 1))
                ins.then_inc(tok_mm, 1)
            pe.wait_ge(act_done, 1)
            pe.wait_ge(ld_wp, 16)
            for b in range(B):
                p, odd = divmod(b, 2)
                ins = pe.matmul(bank[2][64 * odd:64 * odd + 64, 128 * p:128 * (p + 1)], g_sb[:, N_IMG * b:N_IMG * (b + 1)], W("w3"), start=True, stop=True)
            ins.then_inc(h_mm, 1)

            def transposes(n):
                pe.wait_ge(hn_ready, 4 * (n + 1))
                for i in range(4):
                    ins = pe.transpose(bank[n % 3][:, 128 * i:128 * (i + 1)], hn[:, 4 * (n % 3) + i, :], ident)
                ins.then_inc(tr_done, 1)

            pe.wait_ge(ld_c, 16)
            for n in range(3):
                transposes(n)

            def wait_bank(item):
                n = misc_no[item]
                if n >= 2:
                    pe.wait_ge(*evacuated(misc_order[n - 2]))

            def proj(p):
                tok = slice(PT * p, PT * (p + 1))
                pe.wait_ge(hnT_done, 3)
                for n in range(4):
                    item = ("proj", p, n)
                    wait_bank(item)
                    w = W("wq" if n < 2 else "wk")[:, 128 * (n % 2):128 * (n % 2) + 128]
                    pe.matmul(mbank(item)[:, 0:PT], w, hnT[:, tok], start=True, stop=True).then_inc(misc_ready, 1)
                item = ("proj", p, 4)
                wait_bank(item)
                for j in range(TJ):
                    ins = pe.matmul(mbank(item)[:, 128 * j:128 * (j + 1)], hnT[:, PT * p + 128 * j:PT * p + 128 * (j + 1)], W("wv"), start=True, stop=True)
                ins.then_inc(misc_ready, 1)

            def score(p, hd, j):
                g = TJ * (HEADS * p + hd) + j
                if g % (TJ * HEADS) == 0:
                    pe.wait_ge(stack_ld[p % NST], 16 * 18 * (p // NST + 1))
                if g >= 2:
                    pe.wait_ge(s_max, g - 1)
                for s in range(2):
                    for r0, rn, bb in batches(j):
                        ins = pe.matmul(bank[g % 2][r0:r0 + rn, SEQ * s:SEQ * (s + 1)],
                                        q_st[p % NST][0:SROWS, 2 * hd + s, 128 * j + r0:128 * j + r0 + rn],
                                        k_st[p % NST][0:SROWS, 2 * hd + s, SEQ * bb:SEQ * (bb + 1)], start=True, stop=True)
                ins.then_inc(s_ready, 1)

            def max_rows(p):
                item = ("max", p, 0)
                pe.wait_ge(s_max, TJ * HEADS * (p + 1))
                wait_bank(item)
                for j in range(TJ):
                    ins = pe.transpose(mbank(item)[0:HS, 128 * j:128 * (j + 1)], smax[:, p % 2, j, :], ident)
                ins.then_inc(misc_ready, 1)

            def score_t(p, hd, j):
                g = TJ * (HEADS * p + hd) + j
                if g % (TJ * HEADS) == 0:
                    pe.wait_ge(max_ld[p % NST], 16 * NPART * (p // NST + 1))
                    pe.wait_ge(ones_done, NST)
                    pe.wait_ge(init_done, 1)
                if g >= 2:
                    pe.wait_ge(exp_done, g - 1)
                for s in range(2):
                    for r0, rn, bb in batches(j):
                        ins = pe.matmul(bank[2 + g % 2][r0:r0 + rn, SEQ * s:SEQ * (s + 1)],
                                        k_st[p % NST][0:SROWS + NPART, 2 * hd + s, 128 * j + r0:128 * j + r0 + rn],
                                        q_st[p % NST][0:SROWS + NPART, 2 * hd + s, SEQ * bb:SEQ * (bb + 1)], start=True, stop=True)
                ins.then_inc(st_ready, 1)

            def weigh(p, hd):
                g = TJ * (HEADS * p + hd)
                pe.wait_ge(exp_done, g + TJ)
                half = 2 * p + hd // 4
                if hd % 4 == 0 and half >= 1:
                    pe.wait_ge(av_free, 2 * half)
                q0 = 32 * (hd % 4)
                for bb in range(2):
                    spans = [(j, r0, rn) for j in range(TJ) for r0, rn, b2 in batches(j) if b2 == bb]
                    for i, (j, r0, rn) in enumerate(spans):
                        ins = pe.matmul(bank[4 + bb][q0:q0 + 32, 0:2 * SEQ], vaug[r0:r0 + rn, TJ * p + j, hd, :],
                                        p_ring[r0:r0 + rn, (g + j) % NPT, :, :].rearrange("p s q -> p (s q)"),
                                        start=(i == 0), stop=(i == len(spans) - 1))
                ins.then_inc(av_done, 1)

            def out_rows(p):
                pe.wait_ge(av_free, 4 * (p + 1))
                for j in range(TJ):
                    item = ("out", p, j)
                    wait_bank(item)
                    for hg in range(2):
                        for s in range(2):
                            c = 128 * (2 * hg + s)
                            ins = pe.transpose(mbank(item)[:, c:c + 128], oT[:, hg, s, 128 * j:128 * (j + 1)], ident)
                    ins.then_inc(misc_ready, 1)

            proj(0)
            proj(1)
            for hd in range(HEADS):
                for j in range(TJ):
                    score(0, hd, j)
            max_rows(0)
            for p in range(PAIRS):
                nxt = [(p + 1, a // TJ, a % TJ) for a in range(TJ * HEADS)] if p + 1 < PAIRS else []
                for hd in range(HEADS):
                    ahead = nxt[4 * hd:4 * hd + 4]
                    for j in range(TJ):
                        if ahead:
                            score(*ahead[j])
                        score_t(p, hd, j)
                    if ahead:
                        score(*ahead[3])
                    if hd == 2 and p + 2 < PAIRS:
                        proj(p + 2)
                    if hd == 6 and nxt:
                        max_rows(p + 1)
                    if hd >= 1:
                        weigh(p, hd - 1)
                weigh(p, HEADS - 1)
                out_rows(p)

            for n in range(3, 6):
                transposes(n)
            for t in range(T):
                if t % 4 == 0:
                    pe.wait_ge(hnT_done, 4 + t // 4)
                if t == 0:
                    pe.wait_ge(out_read, TJ * PAIRS)
                ins = pe.matmul(bank[7][:, E * t:E * (t + 1)], hnT[:, 128 * t:128 * (t + 1)], W("gate"), start=True, stop=True)
            ins.then_inc(lg_mm, 1)

            def sh_hidden(k):
                tc, ic = divmod(k, IC)
                if k >= 4:
                    pe.wait_ge(sh_act, k - 3)
                pe.matmul(bank[k % 4][:, :], W("sw1")[:, 128 * ic:128 * (ic + 1)], hnT[:, 512 * tc:512 * (tc + 1)], start=True, stop=True)\
                    .then_inc(sh_mm, 1)

            def sh_out(tc):
                pe.wait_ge(sh_act, IC * (tc + 1))
                if tc >= 2:
                    pe.wait_ge(sh_add, tc - 1)
                for i in range(4):
                    for ic in range(IC):
                        ins = pe.matmul(bank[4 + tc % 2][:, 128 * i:128 * (i + 1)], a_sh[:, tc % 2, ic, 128 * i:128 * (i + 1)],
                                        W("sw2")[:, D * ic:D * (ic + 1)], start=(ic == 0), stop=(ic == IC - 1))
                ins.then_inc(sh_y, 1)

            for k in range(4):
                sh_hidden(k)
            pe.wait_ge(oh_done, 1)
            for t in range(T):
                for u in range(t + 1):
                    pe.matmul(bank[7][:, E * t:E * (t + 1)], tri_b[:, :] if u == t else ones_b[:, :], oh_b[:, u, :], start=(u == 0), stop=(u == t))
            for u in range(T):
                ins = pe.matmul(bank[7][:, 128:128 + E], ones_b[:, :], oh_b[:, u, :], start=(u == 0), stop=(u == T - 1))
            ins.then_inc(rank_mm, 1)
            for k in range(4, 8):
                sh_hidden(k)
            sh_out(0)
            for k in range(8, 12):
                sh_hidden(k)
            sh_out(1)
            sh_out(2)

            def turn_x(t):
                pe.wait_ge(xs_ld[t % NX], 16 * (t // NX + 1))
                if t >= 1:
                    pe.wait_ge(x_cp, t)
                else:
                    pe.wait_ge(sh_add, 2)
                pe.transpose(bank[5][:, 0:D], xs[:, t % NX, :], ident).then_inc(x_tr, 1)

            def up(t, e, m):
                pe.wait_ge(x_cp, t + 1)
                if m == 0 and t >= 2:
                    pe.wait_ge(silu_done, t - 1)
                if m == 1 and t >= 2:
                    pe.wait_ge(gated, t - 1)
                pe.matmul(bank[2 * m + t % 2][:, :], xsT[:, t % 2, :], w13_sb[:, bass.ds(e, 1), m, :].rearrange("p a i -> p (a i)"), start=True, stop=True)\
                    .then_inc(up_b if m else up_a, 1)

            def turn_g(t):
                pe.wait_ge(gated, t + 1)
                if t >= 1:
                    pe.wait_ge(g_cp, t)
                else:
                    pe.wait_ge(sh_add, 3)
                for c in range(IC):
                    ins = pe.transpose(bank[4][:, 128 * c:128 * (c + 1)], gate_sb[:, t % 2, 128 * c:128 * (c + 1)], ident)
                ins.then_inc(g_tr, 1)

            def down(t, e):
                pe.wait_ge(g_cp, t + 1)
                if t >= 2:
                    pe.wait_ge(y_cp, t - 1)
                for c in range(IC):
                    ins = pe.matmul(bank[6 + t % 2][:, 0:D], gT[:, t % 2, 128 * c:128 * (c + 1)],
                                    w2_sb[:, bass.ds(e, 1), c, :].rearrange("p a d -> p (a d)"), start=(c == 0), stop=(c == IC - 1))
                ins.then_inc(y_mm, 1)

            pe.wait_ge(ld_exp, 16 * 2 * E)
            pe.wait_ge(et_done, 1)
            pe.wait_ge(sh_act, 3 * IC)
            turn_x(0)
            prev = None
            for t in range(SLOT_TILES):
                e = pe.value_load(et_i[0:1, t:t + 1], min_val=0, max_val=E - 1)
                up(t, e, 0)
                if t >= 1:
                    turn_g(t - 1)
                up(t, e, 1)
                if t + 1 < SLOT_TILES:
                    turn_x(t + 1)
                if t >= 1:
                    down(t - 1, prev)
                prev = e
            turn_g(SLOT_TILES - 1)
            down(SLOT_TILES - 1, prev)


def layouts(inputs):
    a = {k: np.ascontiguousarray(v) for k, v in inputs.items()}
    g = lambda n: a["L0_" + n]
    f32 = np.float32
    x = a["x"].reshape(B, SIDE, PATCH, SIDE, PATCH).transpose(2, 4, 0, 1, 3).reshape(KC, 128, B * N_IMG).transpose(1, 0, 2)
    wn = np.stack([g("tok_" + n).T.reshape(KC, 128, 128).transpose(1, 0, 2) for n in ("W1_w", "W1_sw", "W2_w", "W2_sw")], axis=1)

    def heads(w):
        return w.reshape(-1, 2, HSC, DH).transpose(0, 1, 3, 2).reshape(-1, 2 * D)

    col = lambda v: v.reshape(-1, 128).T
    n = dict(ei1=col(g("tok_eps_in1")), ei2=col(g("tok_eps_in2")), eo1=col(g("tok_eps_out1")), eo2=col(g("tok_eps_out2")),
             b1=col(g("tok_W1_b")), sb1=col(g("tok_W1_sb")), b2=col(g("tok_W2_b")), sb2=col(g("tok_W2_sb")),
             bq=col(heads(g("attn_bq"))), bk=col(heads(g("attn_bk"))))
    npack = np.concatenate([n[k] for k in N_COLS], axis=1)
    rows = np.stack([g("tok_eps_out1"), g("tok_eps_out2"), g("tok_W3_b"), g("attn_bv")])[None]
    w = dict(wq=heads(g("attn_Wq")), wk=heads(g("attn_Wk")), wv=g("attn_Wv"), w3=g("tok_W3_w").T, sw1=g("ffn_sw1").T,
             sw2=g("ffn_sw2").T.reshape(IC, 128, D).transpose(1, 0, 2).reshape(128, IC * D), gate=g("ffn_gate_w").T)
    wpack = np.concatenate([w[k] for k in W_COLS], axis=1)
    w13 = np.stack([g("ffn_w1").transpose(0, 2, 1), g("ffn_w3").transpose(0, 2, 1)], axis=2)
    w2 = g("ffn_w2").transpose(0, 2, 1).reshape(E, IC, 128, D).transpose(0, 2, 1, 3)
    pos = np.arange(N_IMG, dtype=f32)[:, None]
    div = np.exp(np.arange(0, D, 2, dtype=f32) * f32(-math.log(10000.0) / D))
    ang = pos * div
    pe = np.stack([np.sin(ang), np.cos(ang)], axis=-1).reshape(N_IMG, D).astype(f32)
    c = dict(ident=np.eye(128, dtype=f32), tri=np.triu(np.ones((128, 128), f32), 1), ones=np.ones((128, 128), f32),
             pe=np.concatenate([pe, pe]), tile_no=np.tile(np.arange(SLOT_TILES, dtype=f32), (128, 1)),
             prio=np.tile(np.arange(E, 0, -1).astype(f32), (128, 1)))
    cpack = np.concatenate([c[k] for k in C_COLS], axis=1)
    return {k: np.ascontiguousarray(v) for k, v in dict(xT=x, txt=a["txt"], wn=wn, npack=npack, rows=rows, wpack=wpack,
                                                        cpack=cpack, w13=w13, w2=w2).items()}


def kernel(**inputs):
    import concourse.bacc as bacc
    from concourse.bass_utils import run_bass_kernel_spmd

    nc = bacc.Bacc("TRN2", target_bir_lowering=False, num_devices=1)
    arrays, args = {}, []
    for name, a in layouts(inputs).items():
        arrays[f"in_{name}_dram"] = a
        args.append(nc.dram_tensor(f"in_{name}_dram", a.shape, mybir.dt.from_np(a.dtype), kind="ExternalInput").ap())
    o = nc.dram_tensor("out_dram", (B * SEQ, D), mybir.dt.float32, kind="ExternalOutput").ap()
    build_kernel(nc, *args, o)
    r = run_bass_kernel_spmd(nc, [arrays], core_ids=[0])
    return r.results[0]["out_dram"].reshape(B, SEQ, D)
```

```python
import math

import numpy as np

import concourse.bass as bass
from concourse import mybir
from contextlib import ExitStack

B, IMG_SIDE, PATCH = 8, 128, 16
SIDE = IMG_SIDE // PATCH
N_IMG, N_TXT = SIDE * SIDE, 128
SEQ = N_IMG + N_TXT
D = 128
T = B * SEQ // 128
PAIRS = B // 2
TJ = 3
PT = TJ * 128
HEADS, DH = 8, 16
HS = 2 * HEADS
HSC = 8
LAM = 0.5
KC = PATCH * PATCH // 128
E, I = 8, 512
IC = I // 128
SLOT_TILES = (B * SEQ + E * 127) // 128
EPS = 1e-5
NPART = 3
K_PARTS = (0, 1, 2, 0, 1, 0)
Q_PARTS = (0, 0, 0, 1, 1, 2)
SROWS = 16 * len(K_PARTS)
SHALF = SEQ - 128

W_COLS = dict(wq=2 * D, wk=2 * D, wv=D, w3=D, sw1=I, sw2=IC * D, gate=E)
C_COLS = dict(ident=128, tri=128, ones=128, pe=128, tile_no=SLOT_TILES, prio=E, token=T)
XW = D + 1
NO_TOKEN = 4096.0
HALF_TOK = B * N_IMG // 2
N_COLS = dict(ei1=KC, ei2=KC, eo1=1, eo2=1, b1=1, sb1=1, b2=1, sb2=1, bq=2, bk=2)


def columns(cols):
    at, out = 0, {}
    for name, n in cols.items():
        out[name] = slice(at, at + n)
        at += n
    return out, at


def build_kernel(nc, xT, txt, wn, npack, rows, wpack, cpack, w13, w2, out):
    F32, BF16 = mybir.dt.float32, mybir.dt.bfloat16
    I32, U32 = mybir.dt.int32, mybir.dt.uint32
    ALU, ACT, AX = mybir.AluOpType, mybir.ActivationFunctionType, mybir.AxisListType
    WC, WN = columns(W_COLS)
    CC, CN = columns(C_COLS)
    NC_, NN = columns(N_COLS)

    split_dram = nc.dram_tensor("split_scratch", [4 * PAIRS, NPART, 128, PT], BF16, kind="Internal").ap()
    xs_dram = nc.dram_tensor("xs_scratch", [SLOT_TILES * 128, XW], F32, kind="Internal").ap()
    base_dram = nc.dram_tensor("base_scratch", [B * SEQ, D], F32, kind="Internal").ap()

    ctx = ExitStack()
    with ctx:
        def sb(name, shape, dt=F32):
            return ctx.enter_context(nc.sbuf_tensor(name, shape, dt))

        def sem(name):
            return ctx.enter_context(nc.semaphore(name))

        bank = [ctx.enter_context(nc.psum_tensor(f"bank{i}", [128, 512], F32)) for i in range(8)]

        NST = 3
        SF = HS * PT // 2
        stacks = sb("stacks", [128, 2 * NST * 2 * SF], BF16)
        words = stacks[:, :].bitcast(F32)
        free_q = words[:, 4 * SF:5 * SF]
        free_k = words[:, 5 * SF:6 * SF]
        assert E * (2 * I + IC * D) <= 4 * SF
        w13_sb = words[:, 2 * SF:2 * SF + E * 2 * I].rearrange("p (e m i) -> p e m i", e=E, m=2)
        w2_sb = words[:, 2 * SF + E * 2 * I:2 * SF + E * (2 * I + IC * D)].rearrange("p (e c d) -> p e c d", e=E, c=IC)
        x_sb = free_k[:, 0:1024].rearrange("p (c t) -> p c t", c=KC)
        wn_sb = free_k[:, 1024:2048].rearrange("p (m c n) -> p m c n", m=4, c=KC)
        np_sb = sb("np_sb", [128, NN])
        rows_sb = sb("rows_sb", [128, 2, 128])
        wp_sb = sb("wp_sb", [128, WN])
        c_sb = sb("c_sb", [128, CN])

        def W(name):
            return wp_sb[:, WC[name]]

        def C(name):
            return c_sb[:, CC[name]]

        def N(name):
            return np_sb[:, NC_[name]]

        ident = C("ident")

        noise = sb("noise", [128, 6])
        nz_abs, nz_y, nz_u = [sb(f"nz{i}", [128, 6]) for i in range(3)]
        diag = sb("diag", [128, 2, 128])
        wt = free_k[:, 2048:2304].rearrange("p (c n) -> p c n", c=KC)
        w1n = free_k[:, 2304:2560].rearrange("p (c n) -> p c n", c=KC)
        w2n = free_k[:, 2560:2816].rearrange("p (c n) -> p c n", c=KC)
        bn_ = sb("bn_", [128, 2])
        bq4 = sb("bq4", [128, 2])
        peb = sb("peb", [128, 128])
        g_sb = free_q[:, 0:512]
        inner = free_q[:, 512:1024]
        gm = free_q[:, 1024:1536]
        ex = free_q[:, 1536:2048]
        mu = free_q[:, 2048:2560]
        mr = free_q[:, 2560:3072]

        h = sb("h", [128, T, D])
        hn = sb("hn", [128, T, XW])
        hnT = sb("hnT", [128, T * 128])
        stats = sb("stats", [128, T, 6])
        mv = sb("mv", [128, T, 2])
        ve = sb("ve", [128, T])
        rstd = sb("rstd", [128, T])
        ln_u = sb("ln_u", [128, T])

        NF = 4
        f_ring = sb("f_ring", [128, NF, PT])
        r1, r1v = sb("r1", [128, PT]), sb("r1v", [128, PT])
        parts = sb("parts", [128, NF, NPART, PT], BF16)
        q_st, k_st = [[stacks[:, (2 * i + m) * 2 * SF:(2 * i + m + 1) * 2 * SF].rearrange("p (g t) -> p g t", g=HS) for i in range(NST)] for m in range(2)]
        vaug = sb("vaug", [128, T, HEADS, 32])
        smax = sb("smax", [128, 2, TJ, HS])
        mx_f = sb("mx_f", [HSC, PT])
        mx_r = sb("mx_r", [HSC, PT])
        mx_p = sb("mx_p", [HSC, 2, NPART, PT], BF16)
        GH = TJ * HEADS // 2
        p_ring = sb("p_ring", [128, 2, GH, 2, SEQ])
        oT = sb("oT", [128, 2, 2, PT])
        rs = sb("rs", [128, TJ, HS])
        o1 = sb("o1", [128, TJ, HS, DH])
        o2 = sb("o2", [128, TJ * D])

        lg = sb("lg", [128, T, E])
        mxl = sb("mxl", [128, T])
        oh = sb("oh", [128, T, E])
        oh_b = sb("oh_b", [128, T, E], BF16)
        tri_b = sb("tri_b", [128, 128], BF16)
        ones_b = sb("ones_b", [128, 128], BF16)
        cnt = sb("cnt", [128, E])
        cnt_i = sb("cnt_i", [128, E], I32)
        tiles_e = sb("tiles_e", [128, E])
        incl = sb("incl", [128, E])
        base = sb("base", [128, E])
        one8 = sb("one8", [128, E])
        slot_f = sb("slot_f", [128, T])
        slot_u = sb("slot_u", [128, T], U32)
        cmp = sb("cmp", [128, SLOT_TILES, E])
        et_f = sb("et_f", [128, SLOT_TILES])
        et_i = sb("et_i", [128, SLOT_TILES], I32)
        empty = sb("empty", [128, XW])
        spaces = {"stack": [words, 0], "exp": [p_ring[:, :, :, :, :].rearrange("p a g s q -> p (a g s q)"), 0]}

        def carve(where, *shape):
            space, at = spaces[where]
            n = math.prod(shape)
            spaces[where][1] += n
            v = space[:, at:at + n]
            names = "abc"[:len(shape)]
            return v.rearrange(f"p ({' '.join(names)}) -> p {' '.join(names)}", **dict(zip(names, shape)))

        a_sh = carve("stack", 2, IC, 512)
        NX = 3
        xs = carve("exp", NX, XW)
        xsT = carve("exp", 2, D)
        sA = carve("stack", 2, I)
        gate_sb = carve("stack", 2, I)
        gT = carve("exp", 2, I)
        NY = 3
        y_sb = carve("exp", NY, D)
        y_base = carve("exp", NY, D)
        id_u = sb("id_u", [128, SLOT_TILES], U32)
        assert spaces["stack"][1] <= 2 * SF

        ld_x, ld_wn, ld_rows, ld_wp, ld_c, ld_txt, ld_np = [sem(f"ld_{n}") for n in ("x", "wn", "rows", "wp", "c", "txt", "np")]
        ld_exp = sem("ld_exp")
        dve_step, pool_step, act_step = sem("dve_step"), sem("pool_step"), sem("act_step")
        noise_done, diag_done, eo_mm = sem("noise_done"), sem("diag_done"), sem("eo_mm")
        noisy = sem("noisy")
        tok_mm = sem("tok_mm")
        gm_done = sem("gm_done")
        ex_done = sem("ex_done")
        act_done = sem("act_done")
        h_mm = sem("h_mm")
        hn_ready = sem("hn_ready")
        tr_done = sem("tr_done")
        hnT_done = sem("hnT_done")
        bq_done = sem("bq_done")
        misc_ready = sem("misc_ready")
        out_read = sem("out_read")
        f_done = sem("f_done")
        hi_done = sem("hi_done")
        split_done = [sem(f"split_done{i}") for i in range(NF)]
        split_wr = [sem(f"split_wr{i}") for i in range(NF)]
        stack_ld = [[sem(f"stack_ld{i}{c}") for c in range(2)] for i in range(NST)]
        max_ld = [[sem(f"max_ld{i}{c}") for c in range(2)] for i in range(NST)]
        init_done = sem("init_done")
        ones_done = sem("ones_done")
        v_done = sem("v_done")
        s_ready, s_max = sem("s_ready"), sem("s_max")
        mx_evac, mx_hi, mx_split = sem("mx_evac"), sem("mx_hi"), sem("mx_split")
        st_ready, exp_done = sem("st_ready"), sem("exp_done")
        av_done, av_free = sem("av_done"), [sem("av_free0"), sem("av_free1")]
        lg_mm, oh_done, rank_mm, slot_done, et_done = [sem(n) for n in ("lg_mm", "oh_done", "rank_mm", "slot_done", "et_done")]
        zero_done, xs_zeroed, scattered = sem("zero_done"), sem("xs_zeroed"), sem("scattered")
        sh_mm, sh_act, sh_y, sh_add = [sem(n) for n in ("sh_mm", "sh_act", "sh_y", "sh_add")]
        xs_ld = [sem(f"xs_ld{i}") for i in range(NX)]
        x_tr, x_cp, up_a, up_b, silu_done, gated, g_tr, g_cp, y_mm, y_cp = [sem(n) for n in (
            "x_tr", "x_cp", "up_a", "up_b", "silu_done", "gated", "g_tr", "g_cp", "y_mm", "y_cp")]
        id_done, base_clear, base_st = sem("id_done"), sem("base_clear"), sem("base_st")
        based = [sem(f"based{i}") for i in range(NY)]
        stored = [sem(f"stored{i}") for i in range(NY)]

        def proj_items(p):
            return [("proj", p, n) for n in range(5)]

        misc_order = proj_items(0) + proj_items(1) + [("max", 0, 0), ("max", 0, 1)]
        for p in range(PAIRS):
            misc_order += proj_items(p + 2) if p + 2 < PAIRS else []
            misc_order += [("max", p + 1, 0)] if p + 1 < PAIRS else []
            misc_order += [("out", p - 1, j) for j in range(TJ)] if p >= 1 else []
            misc_order += [("max", p + 1, 1)] if p + 1 < PAIRS else []
        misc_order += [("out", PAIRS - 1, j) for j in range(TJ)]
        misc_no = {item: n for n, item in enumerate(misc_order)}

        SH_BANKS, SY_BANKS = (2, 3, 6, 7), (5, 0, 5)
        UP_BANKS, GT_BANK, XT_BANK, Y_BANKS, RANK_BANK = ((2, 3), (6, 7)), 1, 4, (5, 0), 4

        def mbank(item):
            return bank[6 + misc_no[item] % 2]

        def evacuated(item):
            kind, p, n = item
            if kind == "proj":
                return (f_done, 4 * p + n + 1) if n < 4 else (v_done, p + 1)
            return (mx_evac, 2 * p + n + 1) if kind == "max" else (out_read, TJ * p + n + 1)

        def batches(j):
            return {0: [(0, 128, 0)], 1: [(0, SHALF, 0), (SHALF, 128 - SHALF, 1)], 2: [(0, 128, 1)]}[j]

        block = ctx.enter_context(nc.Block())

        @block.sync
        def _(sp):
            sp.dma_start(np_sb[:, :], npack).then_inc(ld_np, 16)
            sp.dma_start(c_sb[:, :], cpack).then_inc(ld_c, 16)
            sp.dma_start(wn_sb, wn).then_inc(ld_wn, 16)
            sp.dma_start(x_sb, xT).then_inc(ld_x, 16)
            sp.dma_start(rows_sb[:, :, :], rows.to_broadcast([128, 2, 128])).then_inc(ld_rows, 16)
            sp.dma_start(wp_sb[:, :], wpack).then_inc(ld_wp, 16)
            for b in range(B):
                p, odd = divmod(b, 2)
                if odd:
                    sp.dma_start(h[:, TJ * p + 2, :], txt[b, :, :]).then_inc(ld_txt, 16)
                else:
                    sp.dma_start(h[N_IMG:128, TJ * p, :], txt[b, 0:128 - N_IMG, :]).then_inc(ld_txt, 16)
                    sp.dma_start(h[0:SHALF, TJ * p + 1, :], txt[b, 128 - N_IMG:128, :]).then_inc(ld_txt, 16)

            def store_parts(r):
                sp.wait_ge(split_done[r % NF], r // NF + 1)
                sp.dma_start(split_dram[r, :, :, :].rearrange("s x t -> x s t"), parts[:, r % NF, :, :])\
                    .then_inc(split_wr[r % NF], 16)

            def load_stacks(p):
                b = p % NST
                if p >= NST:
                    sp.wait_ge(st_ready, TJ * HEADS * (p - NST + 1))
                for n in range(4):
                    r, ch = 4 * p + n, n // 2
                    if n % 2 == 0:
                        st, blocks = q_st[b], [(j, 1, s) for j, s in enumerate(Q_PARTS)]
                    else:
                        st, blocks = k_st[b], [(0, 3, 0), (3, 2, 0), (5, 1, 0)]
                    sp.wait_ge(split_wr[r % NF], 16 * (r // NF + 1))
                    src = split_dram[r, :, :, :].rearrange("s (d g) t -> (s d) (g t)", g=HSC)
                    for j, m, s in blocks:
                        sp.dma_start(st[16 * j:16 * (j + m), HSC * ch:HSC * (ch + 1), :].rearrange("p g t -> p (g t)"),
                                     src[16 * s:16 * (s + m), :]).then_inc(stack_ld[b][ch], 16)

            def load_max(p, ch):
                b = p % NST
                sp.wait_ge(mx_split, 2 * p + ch + 1)
                for s in range(NPART):
                    sp.dma_start(q_st[b][SROWS + s:SROWS + s + 1, HSC * ch:HSC * (ch + 1), :], mx_p[:, ch, s, :])\
                        .then_inc(max_ld[b][ch], 16)

            for p in range(2):
                for n in range(4):
                    store_parts(4 * p + n)
                load_stacks(p)
            for ch in range(2):
                load_max(0, ch)
            sp.wait_ge(zero_done, 1)
            for t in range(SLOT_TILES):
                sp.dma_start(xs_dram[128 * t:128 * (t + 1), :], empty[:, :]).then_inc(xs_zeroed, 16)
            for p in range(1, PAIRS):
                if p + 1 < PAIRS:
                    for n in range(4):
                        store_parts(4 * (p + 1) + n)
                    load_stacks(p + 1)
                for ch in range(2):
                    load_max(p, ch)
            sp.wait_ge(st_ready, TJ * HEADS * (PAIRS - 1))
            for e in range(E):
                sp.dma_start(w13_sb[:, e, :, :], w13[e, :, :, :]).then_inc(ld_exp, 16)
                sp.dma_start(w2_sb[:, e, :, :], w2[e, :, :, :]).then_inc(ld_exp, 16)

            def load_xs(t):
                if t >= NX:
                    sp.wait_ge(x_tr, t - NX + 1)
                    sp.wait_ge(id_done, t - NX + 1)
                sp.dma_start(xs[:, t % NX, :], xs_dram[128 * t:128 * (t + 1), :]).then_inc(xs_ld[t % NX], 16)

            base_v = base_dram.rearrange("(t p) d -> p t d", p=128)
            for tc in range(2):
                sp.wait_ge(sh_add, tc + 1)
                sp.dma_start(base_v[:, 4 * tc:4 * tc + 4, :], h[:, 4 * tc:4 * tc + 4, :]).then_inc(base_st, 16)
            sp.wait_ge(scattered, 16 * T)
            for t in range(NX):
                load_xs(t)
            sp.wait_ge(sh_add, 3)
            sp.dma_start(base_v[:, 8:12, :], h[:, 8:12, :]).then_inc(base_st, 16)
            for t in range(NX, SLOT_TILES):
                load_xs(t)

        @block.gpsimd
        def _(pool):
            steps = [0]

            def link(ins):
                steps[0] += 1
                ins.then_inc(pool_step, 1)
                pool.wait_ge(pool_step, steps[0])

            link(pool.memset(empty[:, 0:D], 0.0))
            pool.memset(empty[:, D:XW], NO_TOKEN).then_inc(zero_done, 1)
            pool.wait_ge(zero_done, 1)
            def ones_rows(b):
                if b == NST - 1:
                    pool.wait_ge(h_mm, 2)
                pool.memset(k_st[b][SROWS:SROWS + NPART, :, :], 1.0).then_inc(ones_done, 1)
                pool.wait_ge(ones_done, b + 1)

            def split(r):
                pool.wait_ge(f_done, r + 1)
                pool.wait_ge(hi_done, r + 1)
                f, pr = f_ring[:, r % NF, :], parts[:, r % NF, :, :]
                link(pool.tensor_tensor(r1[:, :], f, pr[:, 0, :], ALU.subtract))
                link(pool.tensor_scalar(pr[:, 1, :], r1[:, :], 1.0, 0.0, ALU.mult, ALU.add))
                pool.tensor_tensor(pr[:, 2, :], r1[:, :], pr[:, 1, :], ALU.subtract).then_inc(split_done[r % NF], 1)
                pool.wait_ge(split_done[r % NF], r // NF + 1)

            def split_max(p, ch):
                pool.wait_ge(mx_evac, 2 * p + ch + 1)
                pool.wait_ge(mx_hi, 2 * p + ch + 1)
                mp = mx_p[:, ch, :, :]
                link(pool.tensor_tensor(mx_r[:, :], mx_f[:, :], mp[:, 0, :], ALU.subtract))
                link(pool.tensor_scalar(mp[:, 1, :], mx_r[:, :], 1.0, 0.0, ALU.mult, ALU.add))
                pool.tensor_tensor(mp[:, 2, :], mx_r[:, :], mp[:, 1, :], ALU.subtract).then_inc(mx_split, 1)
                pool.wait_ge(mx_split, 2 * p + ch + 1)

            ones_rows(0)
            ones_rows(1)
            for r in (0, 2, 4, 5, 6, 7):
                split(r)
            ones_rows(2)
            for ch in range(2):
                split_max(0, ch)
            for p in range(1, PAIRS):
                if p + 1 < PAIRS:
                    for n in range(4):
                        split(4 * (p + 1) + n)
                for ch in range(2):
                    split_max(p, ch)

            pool.wait_ge(slot_done, 1)
            pool.wait_ge(xs_zeroed, 16 * SLOT_TILES)
            for t in range(T):
                pool.indirect_dma_start(out=xs_dram, out_offset=bass.IndirectOffsetOnAxis(ap=slot_u[:, t:t + 1], axis=0),
                                        in_=hn[:, t, :], in_offset=None).then_inc(scattered, 16)

            def index(t):
                return bass.IndirectOffsetOnAxis(ap=id_u[:, t:t + 1], axis=0)

            def gather_base(t):
                pool.wait_ge(id_done, t + 1)
                if t == 0:
                    pool.wait_ge(base_st, 16 * 3)
                    pool.wait_ge(base_clear, 1)
                if t >= NY:
                    pool.wait_ge(y_cp, t - NY + 1)
                pool.indirect_dma_start(out=y_base[:, t % NY, :], out_offset=None, in_=base_dram, in_offset=index(t),
                                        bounds_check=B * SEQ - 1, oob_is_err=False).then_inc(based[t % NY], 16)

            gather_base(0)
            gather_base(1)
            for t in range(SLOT_TILES):
                pool.wait_ge(y_cp, t + 1)
                pool.indirect_dma_start(out=out, out_offset=index(t), in_=y_sb[:, t % NY, :], in_offset=None,
                                        bounds_check=B * SEQ - 1, oob_is_err=False).then_inc(stored[t % NY], 16)
                if t + 2 < SLOT_TILES:
                    gather_base(t + 2)
            for i in range(NY):
                pool.wait_ge(stored[i], 16 * len(range(i, SLOT_TILES, NY)))

        @block.scalar
        def _(act):
            for half in range(2):
                act.wait_ge(gm_done, half + 1)
                c = slice(HALF_TOK * half, HALF_TOK * (half + 1))
                act.activation(ex[:, c], gm[:, c], ACT.Exp).then_inc(ex_done, 1)

            def copy_hnT(n):
                act.wait_ge(tr_done, n + 1)
                c = PT * (n % PAIRS)
                act.activation(hnT[:, c:c + PT], bank[n % 2][:, 0:PT], ACT.Copy).then_inc(hnT_done, 1)

            def evac_proj(p):
                for n in range(4):
                    r = 4 * p + n
                    item = ("proj", p, n)
                    act.wait_ge(misc_ready, misc_no[item] + 1)
                    if r >= NF:
                        act.wait_ge(split_done[r % NF], r // NF)
                    bias = N("bk")[:, n // 2:n // 2 + 1] if n % 2 else bq4[:, n // 2:n // 2 + 1]
                    act.activation(f_ring[:, r % NF, :], mbank(item)[:, 0:PT], ACT.Identity, bias=bias,
                                   scale=1.0 if n % 2 else DH ** -0.5).then_inc(f_done, 1)

            def evac_max(p, ch):
                item = ("max", p, ch)
                act.wait_ge(misc_ready, misc_no[item] + 1)
                if p >= 1:
                    act.wait_ge(max_ld[(p - 1) % NST][ch], 16 * NPART * ((p - 1) // NST + 1))
                if p + ch >= 1:
                    act.wait_ge(mx_split, 2 * p + ch)
                act.activation(mx_f[:, :], mbank(item)[0:HSC, 0:PT], ACT.Copy).then_inc(mx_evac, 1)
                act.wait_ge(mx_evac, 2 * p + ch + 1)
                act.activation(mx_p[:, ch, 0, :], mx_f[:, :], ACT.Copy).then_inc(mx_hi, 1)

            def exp(p, hd, j):
                g = TJ * (HEADS * p + hd) + j
                act.wait_ge(st_ready, g + 1)
                half = g // GH
                if half >= 2:
                    act.wait_ge(av_done, 4 * (half - 1))
                act.activation(p_ring[:, half % 2, g % GH, :, :], bank[2 + g % 2][:, 0:2 * SEQ].rearrange("p (s q) -> p s q", s=2),
                               ACT.Exp).then_inc(exp_done, 1)

            def evac_av(half, bb):
                act.wait_ge(av_done, 4 * half + 2 * (bb + 1))
                if half >= 2 and half % 2 == 0 and bb == 0:
                    act.wait_ge(misc_ready, misc_no[("out", half // 2 - 1, TJ - 1)] + 1)
                act.activation(oT[:, half % 2, :, SEQ * bb:SEQ * (bb + 1)],
                               bank[4 + bb][:, 0:2 * SEQ].rearrange("p (s q) -> p s q", s=2), ACT.Copy).then_inc(av_free[bb], 1)

            copy_hnT(0)
            act.wait_ge(bq_done, 1)
            evac_proj(0)
            copy_hnT(1)
            evac_proj(1)
            copy_hnT(2)
            copy_hnT(3)
            evac_max(0, 0)
            evac_max(0, 1)
            for p in range(PAIRS):
                for hd in range(HEADS):
                    half = 2 * p + hd // 4
                    for j in range(TJ):
                        exp(p, hd, j)
                    if hd % 4 == 0 and half >= 2:
                        evac_av(half - 2, 1)
                    if hd % 4 == 2 and half >= 1:
                        evac_av(half - 1, 0)
                    if hd == 2 and p + 2 < PAIRS:
                        evac_proj(p + 2)
                    if hd == 3 and p + 1 < PAIRS:
                        evac_max(p + 1, 0)
                    if hd == 6 and p + 1 < PAIRS:
                        evac_max(p + 1, 1)
                    if hd in (5, 6) and p == PAIRS - 1:
                        copy_hnT(PAIRS + hd - 5)
            evac_av(2 * PAIRS - 2, 1)
            evac_av(2 * PAIRS - 1, 0)
            evac_av(2 * PAIRS - 1, 1)
            copy_hnT(PAIRS + 2)

            def gelu(k):
                act.wait_ge(sh_mm, k + 1)
                tc, ic = divmod(k, IC)
                if tc >= 2:
                    act.wait_ge(sh_y, tc - 1)
                act.activation(a_sh[:, tc % 2, ic, :], bank[SH_BANKS[k % 4]][:, :], ACT.Gelu).then_inc(sh_act, 1)

            for k in range(4):
                gelu(k)
            copy_hnT(PAIRS + 3)
            for k in range(4, 3 * IC):
                gelu(k)

            def silu(t):
                act.wait_ge(up_a, t + 1)
                if t >= 2:
                    act.wait_ge(gated, t - 1)
                act.activation(sA[:, t % 2, :], bank[UP_BANKS[0][t % 2]][:, :], ACT.Silu).then_inc(silu_done, 1)

            def copy_gT(t):
                act.wait_ge(g_tr, t + 1)
                if t >= 2:
                    act.wait_ge(y_mm, t - 1)
                act.activation(gT[:, t % 2, :], bank[GT_BANK][:, :], ACT.Copy).then_inc(g_cp, 1)

            for t in range(SLOT_TILES):
                silu(t)
                if t >= 1:
                    copy_gT(t - 1)
            copy_gT(SLOT_TILES - 1)

        @block.vector
        def _(dve):
            steps = [0]

            def link(ins):
                steps[0] += 1
                ins.then_inc(dve_step, 1)
                dve.wait_ge(dve_step, steps[0])

            def rsqrt(y, v, u):
                vi, yi = v.bitcast(U32), y.bitcast(I32)
                link(dve.tensor_scalar(y.bitcast(U32), vi, 1, None, ALU.logical_shift_right))
                link(dve.tensor_scalar(yi, yi, -1.0, float(0x5F3759DF), ALU.mult, ALU.add))
                for _ in range(3):
                    link(dve.tensor_tensor(u, v, y, ALU.mult))
                    link(dve.scalar_tensor_tensor(u, u, -0.5, y, ALU.mult, ALU.mult))
                    link(dve.scalar_tensor_tensor(y, u, 1.5, y, ALU.add, ALU.mult))

            dve.wait_ge(ld_np, 16)
            eps = np_sb[:, 0:6]
            link(dve.tensor_scalar(nz_abs[:, :].bitcast(U32), eps.bitcast(U32), 0x7FFFFFFF, None, ALU.bitwise_and))
            rsqrt(nz_y[:, :], nz_abs[:, :], nz_u[:, :])
            link(dve.tensor_tensor(noise[:, :], eps, nz_y[:, :], ALU.mult))
            dve.wait_ge(ld_c, 16)
            for m in range(2):
                dve.tensor_scalar(diag[:, m, :], ident, noise[:, 4 + m:5 + m], None, ALU.mult).then_inc(diag_done, 1)
            dve.wait_ge(ld_wn, 16)
            dve.wait_ge(eo_mm, 1)
            for m, wdst in enumerate((w1n, w2n)):
                for kc in range(KC):
                    ins = dve.scalar_tensor_tensor(wt[:, kc, :], bank[6][:, 128 * m:128 * (m + 1)], noise[:, 2 * m + kc:2 * m + kc + 1],
                                                   wn_sb[:, 2 * m + 1, kc, :], ALU.mult, ALU.mult)
                link(ins)
                dve.tensor_tensor(wdst[:, :, :], wt[:, :, :], wn_sb[:, 2 * m, :, :], ALU.add).then_inc(noisy, 1)
                dve.wait_ge(noisy, m + 1)
            for m, (bb, ss) in enumerate((("b1", "sb1"), ("b2", "sb2"))):
                ins = dve.scalar_tensor_tensor(bn_[:, m:m + 1], N(ss), noise[:, 4 + m:5 + m], N(bb), ALU.mult, ALU.add)
            ins.then_inc(noisy, 1)
            dve.tensor_scalar(bq4[:, :], N("bq"), DH ** -0.5, None, ALU.mult).then_inc(bq_done, 1)
            dve.wait_ge(ld_rows, 16)
            link(dve.tensor_tensor(peb[:, :], C("pe"), rows_sb[:, 0, :], ALU.add))
            dve.tensor_copy(hn[:, :, D], C("token"))

            dve.wait_ge(noisy, 3)
            for half in range(2):
                c = slice(HALF_TOK * half, HALF_TOK * (half + 1))
                dve.wait_ge(tok_mm, 2 * half + 1)
                dve.tensor_scalar(gm[:, c], bank[3 * half][:, 0:HALF_TOK], bn_[:, 0:1], 20.0, ALU.add, ALU.min).then_inc(gm_done, 1)

            def mish(half):
                c = slice(HALF_TOK * half, HALF_TOK * (half + 1))
                dve.wait_ge(tok_mm, 2 * half + 2)
                link(dve.tensor_scalar(inner[:, c], bank[3 * half + 1][:, 0:HALF_TOK], bn_[:, 1:2], None, ALU.add))
                dve.wait_ge(ex_done, half + 1)
                link(dve.scalar_tensor_tensor(mu[:, c], ex[:, c], 2.0, ex[:, c], ALU.add, ALU.mult))
                dve.scalar_tensor_tensor(inner[:, c], bank[3 * half][:, 0:HALF_TOK], bn_[:, 0:1], inner[:, c], ALU.add, ALU.mult)
                link(dve.tensor_scalar(mr[:, c], mu[:, c], 2.0, None, ALU.add))
                link(dve.reciprocal(ex[:, c], mr[:, c]))
                link(dve.tensor_tensor(mu[:, c], mu[:, c], ex[:, c], ALU.mult))
                dve.tensor_tensor(g_sb[:, c], mu[:, c], inner[:, c], ALU.mult).then_inc(act_done, 1)

            hv = h[:, :, :].rearrange("p (a j) d -> p a j d", j=TJ)

            def image_tokens(half):
                dve.wait_ge(h_mm, half + 1)
                n = PAIRS // 2
                for odd in range(2):
                    q = slice(64 * odd, 64 * odd + 64)
                    pb = peb[q, :].rearrange("p (a d) -> p a d", a=1).to_broadcast([64, n, D])
                    link(dve.tensor_tensor(hv[q, n * half:n * (half + 1), odd, :], bank[2 + 3 * half][q, 0:n * D].rearrange("p (a d) -> p a d", a=n), pb, ALU.add))

            def ln_stats(t0, t1):
                for t in range(t0, t1):
                    ins = dve.bn_stats(stats[:, t, :], h[:, t, :])
                link(ins)
                for t in range(t0, t1):
                    ins = dve.bn_aggr(mv[:, t, :], stats[:, t, :])
                link(ins)

            def ln_scale(t0, t1):
                link(dve.tensor_scalar(ve[:, t0:t1], mv[:, t0:t1, 1], EPS, None, ALU.add))
                rsqrt(rstd[:, t0:t1], ve[:, t0:t1], ln_u[:, t0:t1])
                for t in range(t0, t1):
                    dve.tensor_scalar(hn[:, t, 0:D], h[:, t, :], mv[:, t, 0:1], rstd[:, t:t + 1], ALU.subtract, ALU.mult)\
                        .then_inc(hn_ready, 1)

            def high_part(p):
                for n in range(4):
                    r = 4 * p + n
                    f, pr = f_ring[:, r % NF, :], parts[:, r % NF, :, :]
                    dve.wait_ge(f_done, r + 1)
                    if r >= NF:
                        dve.wait_ge(split_wr[r % NF], 16 * (r // NF))
                    dve.tensor_copy(pr[:, 0, :], f).then_inc(hi_done, 1)
                    if r in (1, 3):
                        dve.wait_ge(hi_done, r + 1)
                        link(dve.tensor_tensor(r1v[:, :], f, pr[:, 0, :], ALU.subtract))
                        link(dve.tensor_copy(pr[:, 1, :], r1v[:, :]))
                        dve.tensor_tensor(pr[:, 2, :], r1v[:, :], pr[:, 1, :], ALU.subtract).then_inc(split_done[r % NF], 1)
                item = ("proj", p, 4)
                dve.wait_ge(misc_ready, misc_no[item] + 1)
                bv = rows_sb[:, 1:2, :].rearrange("p a (h d) -> p a h d", d=DH).to_broadcast([128, TJ, HEADS, DH])
                for j in range(TJ):
                    ins = dve.tensor_tensor(vaug[:, TJ * p + j, :, 0:DH], mbank(item)[:, 128 * j:128 * (j + 1)].rearrange("p (h d) -> p h d", d=DH),
                                            bv[:, j, :, :], ALU.add)
                ins.then_inc(v_done, 1)

            def row_max(p, hd, j):
                g = TJ * (HEADS * p + hd) + j
                dve.wait_ge(s_ready, g + 1)
                if p >= 2 and g % (TJ * HEADS) == 0:
                    dve.wait_ge(misc_ready, misc_no[("max", p - 2, 1)] + 1)
                dve.tensor_reduce(smax[:, p % 2, j, 2 * hd:2 * hd + 2], bank[g % 2][:, 0:2 * SEQ].rearrange("p (s k) -> p s k", s=2),
                                  AX.X, ALU.max, negate=True).then_inc(s_max, 1)

            def attn_out(p):
                for j in range(TJ):
                    item = ("out", p, j)
                    dve.wait_ge(misc_ready, misc_no[item] + 1)
                    v = mbank(item)[:, :].rearrange("p (a c) -> p a c", c=32)
                    link(dve.reciprocal(rs[:, j, :], v[:, :, DH]))
                    rv = rs[:, j, :].rearrange("p (a s b) -> p a s b", s=2, b=4)
                    link(dve.tensor_scalar(rv[:, :, 1, :], rv[:, :, 1, :], -LAM, None, ALU.mult))
                    dve.tensor_tensor(o1[:, j, :, :], v[:, :, 0:DH], rs[:, j, :].rearrange("p (a c) -> p a c", c=1).to_broadcast([128, HS, DH]), ALU.mult)\
                        .then_inc(out_read, 1)
                dve.wait_ge(out_read, TJ * (p + 1))
                ov = o1[:, :, :, :].rearrange("p j (a s b) d -> p (j a) s (b d)", s=2, b=4)
                hp = h[:, TJ * p:TJ * (p + 1), :].rearrange("p j (a x) -> p (j a) x", a=2)
                o2v = o2[:, :].rearrange("p (a x) -> p a x", a=2 * TJ)
                link(dve.tensor_tensor(o2v, ov[:, :, 0, :], ov[:, :, 1, :], ALU.add))
                link(dve.tensor_tensor(hp, hp, o2v, ALU.add))
                ln_stats(TJ * p, TJ * (p + 1))

            mish(0)
            image_tokens(0)
            dve.wait_ge(ld_txt, 16 * 3 * PAIRS)
            ln_stats(0, 6)
            ln_scale(0, 6)
            mish(1)
            high_part(0)
            image_tokens(1)
            ln_stats(6, 12)
            ln_scale(6, 12)
            high_part(1)
            dve.tensor_copy(tri_b[:, :], C("tri"))
            dve.tensor_copy(ones_b[:, :], C("ones"))
            dve.memset(one8[:, :], 1.0)
            dve.memset(vaug[:, :, :, DH:DH + 1], 1.0)
            dve.memset(vaug[:, :, :, DH + 1:32], 0.0).then_inc(init_done, 1)
            for hd in range(HEADS):
                for j in range(TJ):
                    row_max(0, hd, j)
            for p in range(PAIRS):
                nxt = [(p + 1, a // TJ, a % TJ) for a in range(TJ * HEADS)] if p + 1 < PAIRS else []
                for hd in range(HEADS):
                    for g in nxt[4 * hd:4 * hd + 4]:
                        row_max(*g)
                    if hd == 2 and p + 2 < PAIRS:
                        high_part(p + 2)
                    if hd == 5 and p == PAIRS - 1:
                        ln_scale(0, 6)
                    if hd == 5 and p >= 1:
                        attn_out(p - 1)
            ln_scale(6, 9)
            attn_out(PAIRS - 1)
            ln_scale(9, 12)

            dve.wait_ge(lg_mm, 1)
            link(dve.tensor_copy(lg[:, :, :], bank[RANK_BANK][:, 0:T * E].rearrange("p (t e) -> p t e", e=E)))
            link(dve.tensor_reduce(mxl[:, :], lg[:, :, :], AX.X, ALU.max))
            def wide(ap):
                return ap.rearrange("p (t a) -> p t a", a=1).to_broadcast([128, T, E])
            def over_tiles(ap):
                return ap.rearrange("p (a e) -> p a e", a=1).to_broadcast([128, T, E])
            link(dve.tensor_tensor(oh[:, :, :], lg[:, :, :], wide(mxl[:, :]), ALU.is_ge))
            link(dve.tensor_tensor(oh[:, :, :], oh[:, :, :], over_tiles(C("prio")), ALU.mult))
            link(dve.tensor_reduce(mxl[:, :], oh[:, :, :], AX.X, ALU.max))
            link(dve.tensor_tensor(oh[:, :, :], oh[:, :, :], wide(mxl[:, :]), ALU.is_equal))
            dve.tensor_copy(oh_b[:, :, :], oh[:, :, :]).then_inc(oh_done, 1)
            dve.wait_ge(rank_mm, 1)
            link(dve.tensor_reduce(cnt[:, :], bank[RANK_BANK][:, 256:256 + T * E].rearrange("p (t e) -> p e t", e=E), AX.X, ALU.add))
            link(dve.tensor_scalar(cnt[:, :], cnt[:, :], 127.0, None, ALU.add))
            link(dve.tensor_copy(cnt_i[:, :], cnt[:, :]))
            link(dve.tensor_scalar(cnt_i[:, :], cnt_i[:, :], 7, None, ALU.arith_shift_right))
            link(dve.tensor_copy(tiles_e[:, :], cnt_i[:, :]))
            link(dve.tensor_tensor_scan(incl[:, :], one8[:, :], tiles_e[:, :], 0.0, ALU.mult, ALU.add))
            link(dve.tensor_tensor(base[:, :], incl[:, :], tiles_e[:, :], ALU.subtract))
            link(dve.tensor_scalar(base[:, :], base[:, :], 128.0, None, ALU.mult))
            link(dve.tensor_tensor(lg[:, :, :], bank[RANK_BANK][:, 128:128 + T * E].rearrange("p (t e) -> p t e", e=E), over_tiles(base[:, :]), ALU.add))
            link(dve.tensor_tensor(lg[:, :, :], lg[:, :, :], oh[:, :, :], ALU.mult))
            link(dve.tensor_reduce(slot_f[:, :], lg[:, :, :], AX.X, ALU.add))
            dve.tensor_copy(slot_u[:, :], slot_f[:, :]).then_inc(slot_done, 1)
            link(dve.tensor_tensor(cmp[:, :, :], incl[:, :].rearrange("p (a e) -> p a e", a=1).to_broadcast([128, SLOT_TILES, E]),
                                   C("tile_no").rearrange("p (t a) -> p t a", a=1).to_broadcast([128, SLOT_TILES, E]), ALU.is_le))
            link(dve.tensor_reduce(et_f[:, :], cmp[:, :, :], AX.X, ALU.add))
            link(dve.tensor_scalar(et_f[:, :], et_f[:, :], E - 1.0, None, ALU.min))
            dve.tensor_copy(et_i[:, :], et_f[:, :]).then_inc(et_done, 1)
            dve.memset(y_base[:, :, :], 0.0).then_inc(base_clear, 1)

            for tc in range(3):
                dve.wait_ge(sh_y, tc + 1)
                hv4 = h[:, 4 * tc:4 * tc + 4, :].rearrange("p t d -> p (t d)")
                dve.tensor_tensor(hv4, bank[SY_BANKS[tc]][:, :], hv4, ALU.add).then_inc(sh_add, 1)

            def take_x(t):
                dve.wait_ge(xs_ld[t % NX], 16 * (t // NX + 1))
                dve.tensor_copy(id_u[:, t:t + 1], xs[:, t % NX, D:XW]).then_inc(id_done, 1)
                dve.wait_ge(x_tr, t + 1)
                if t >= 2:
                    dve.wait_ge(up_b, t - 1)
                dve.tensor_copy(xsT[:, t % 2, :], bank[XT_BANK][:, 0:D]).then_inc(x_cp, 1)

            def gate(t):
                dve.wait_ge(up_b, t + 1)
                dve.wait_ge(silu_done, t + 1)
                if t >= 2:
                    dve.wait_ge(g_tr, t - 1)
                dve.tensor_tensor(gate_sb[:, t % 2, :], bank[UP_BANKS[1][t % 2]][:, :], sA[:, t % 2, :], ALU.mult).then_inc(gated, 1)

            def add_base(t):
                dve.wait_ge(y_mm, t + 1)
                dve.wait_ge(based[t % NY], 16 * (t // NY + 1))
                if t >= NY:
                    dve.wait_ge(stored[t % NY], 16 * (t // NY))
                dve.tensor_tensor(y_sb[:, t % NY, :], bank[Y_BANKS[t % 2]][:, 0:D], y_base[:, t % NY, :], ALU.add).then_inc(y_cp, 1)

            take_x(0)
            for t in range(SLOT_TILES):
                gate(t)
                if t + 1 < SLOT_TILES:
                    take_x(t + 1)
                if t >= 1:
                    add_base(t - 1)
            add_base(SLOT_TILES - 1)

        @block.tensor
        def _(pe):
            pe.wait_ge(ld_c, 16)
            pe.wait_ge(diag_done, 2)
            for m in range(2):
                ins = pe.matmul(bank[6][:, 128 * m:128 * (m + 1)], C("ones"), diag[:, m, :], start=True, stop=True)
            ins.then_inc(eo_mm, 1)
            pe.wait_ge(ld_x, 16)
            for half in range(2):
                for m, wsrc in enumerate((w1n, w2n)):
                    pe.wait_ge(noisy, m + 1)
                    for kc in range(KC):
                        ins = pe.matmul(bank[3 * half + m][:, 0:HALF_TOK], wsrc[:, kc, :], x_sb[:, kc, HALF_TOK * half:HALF_TOK * (half + 1)],
                                        start=(kc == 0), stop=(kc == KC - 1))
                    ins.then_inc(tok_mm, 1)

            def image_tokens(half):
                pe.wait_ge(act_done, half + 1)
                pe.wait_ge(ld_wp, 16)
                for b in range(B // 2):
                    p, odd = divmod(b, 2)
                    at = HALF_TOK * half + N_IMG * b
                    ins = pe.matmul(bank[2 + 3 * half][64 * odd:64 * odd + 64, D * p:D * (p + 1)], g_sb[:, at:at + N_IMG], W("w3"), start=True, stop=True)
                ins.then_inc(h_mm, 1)

            def transposes(n):
                pe.wait_ge(hn_ready, TJ * (n + 1))
                if n >= 2:
                    pe.wait_ge(hnT_done, n - 1)
                if n >= PAIRS and n < PAIRS + 2:
                    pe.wait_ge(s_max, TJ * HEADS * PAIRS)
                for i in range(TJ):
                    ins = pe.transpose(bank[n % 2][:, 128 * i:128 * (i + 1)], hn[:, TJ * (n % PAIRS) + i, 0:D], ident)
                ins.then_inc(tr_done, 1)

            image_tokens(0)

            def wait_bank(item):
                n = misc_no[item]
                if n >= 2:
                    pe.wait_ge(*evacuated(misc_order[n - 2]))

            def proj(p):
                tok = slice(PT * p, PT * (p + 1))
                pe.wait_ge(hnT_done, p + 1)
                for n in range(4):
                    item = ("proj", p, n)
                    wait_bank(item)
                    w = W("wk" if n % 2 else "wq")[:, 128 * (n // 2):128 * (n // 2) + 128]
                    pe.matmul(mbank(item)[:, 0:PT], w, hnT[:, tok], start=True, stop=True).then_inc(misc_ready, 1)
                item = ("proj", p, 4)
                wait_bank(item)
                for j in range(TJ):
                    ins = pe.matmul(mbank(item)[:, 128 * j:128 * (j + 1)], hnT[:, PT * p + 128 * j:PT * p + 128 * (j + 1)], W("wv"), start=True, stop=True)
                ins.then_inc(misc_ready, 1)

            def score(p, hd, j):
                g = TJ * (HEADS * p + hd) + j
                if g == 0:
                    pe.wait_ge(hnT_done, PAIRS)
                if g % GH == 0:
                    pe.wait_ge(stack_ld[p % NST][hd // 4], 16 * 9 * (p // NST + 1))
                if g >= 2:
                    pe.wait_ge(s_max, g - 1)
                for s in range(2):
                    for r0, rn, bb in batches(j):
                        ins = pe.matmul(bank[g % 2][r0:r0 + rn, SEQ * s:SEQ * (s + 1)],
                                        q_st[p % NST][0:SROWS, 2 * hd + s, 128 * j + r0:128 * j + r0 + rn],
                                        k_st[p % NST][0:SROWS, 2 * hd + s, SEQ * bb:SEQ * (bb + 1)], start=True, stop=True)
                ins.then_inc(s_ready, 1)

            def max_rows(p, ch):
                item = ("max", p, ch)
                pe.wait_ge(s_max, TJ * HEADS * p + GH * (ch + 1))
                wait_bank(item)
                for j in range(TJ):
                    ins = pe.transpose(mbank(item)[0:HSC, 128 * j:128 * (j + 1)], smax[:, p % 2, j, HSC * ch:HSC * (ch + 1)], ident)
                ins.then_inc(misc_ready, 1)

            def score_t(p, hd, j):
                g = TJ * (HEADS * p + hd) + j
                if g % GH == 0:
                    pe.wait_ge(max_ld[p % NST][hd // 4], 16 * NPART * (p // NST + 1))
                    pe.wait_ge(ones_done, NST)
                    pe.wait_ge(init_done, 1)
                if g >= 2:
                    pe.wait_ge(exp_done, g - 1)
                for s in range(2):
                    for r0, rn, bb in batches(j):
                        ins = pe.matmul(bank[2 + g % 2][r0:r0 + rn, SEQ * s:SEQ * (s + 1)],
                                        k_st[p % NST][0:SROWS + NPART, 2 * hd + s, 128 * j + r0:128 * j + r0 + rn],
                                        q_st[p % NST][0:SROWS + NPART, 2 * hd + s, SEQ * bb:SEQ * (bb + 1)], start=True, stop=True)
                ins.then_inc(st_ready, 1)

            def weigh(half, c):
                bb, j, r0, rn = ((0, 0, 0, 128), (0, 1, 0, SHALF), (1, 1, SHALF, 128 - SHALF), (1, 2, 0, 128))[c]
                p, hg = divmod(half, 2)
                if c == 0:
                    pe.wait_ge(exp_done, GH * (half + 1))
                if c % 2 == 0 and half >= 1:
                    pe.wait_ge(av_free[bb], half)
                for a in range(4):
                    ins = pe.matmul(bank[4 + bb][32 * a:32 * a + 32, 0:2 * SEQ], vaug[r0:r0 + rn, TJ * p + j, 4 * hg + a, :],
                                    p_ring[r0:r0 + rn, half % 2, TJ * a + j, :, :].rearrange("p s q -> p (s q)"),
                                    start=(c % 2 == 0), stop=(c % 2 == 1))
                ins.then_inc(av_done, 1)

            def out_rows(p):
                for bb in range(2):
                    pe.wait_ge(av_free[bb], 2 * (p + 1))
                for j in range(TJ):
                    item = ("out", p, j)
                    wait_bank(item)
                    for hg in range(2):
                        for s in range(2):
                            c = 128 * (2 * hg + s)
                            ins = pe.transpose(mbank(item)[:, c:c + 128], oT[:, hg, s, 128 * j:128 * (j + 1)], ident)
                    ins.then_inc(misc_ready, 1)

            transposes(0)
            proj(0)
            transposes(1)
            proj(1)
            image_tokens(1)
            transposes(2)
            transposes(3)
            for g in range(TJ * HEADS):
                if g == GH + 3:
                    max_rows(0, 0)
                score(0, g // TJ, g % TJ)
            max_rows(0, 1)
            for p in range(PAIRS):
                nxt = [(p + 1, a // TJ, a % TJ) for a in range(TJ * HEADS)] if p + 1 < PAIRS else []
                for hd in range(HEADS):
                    half = 2 * p + hd // 4
                    ahead = nxt[4 * hd:4 * hd + 4]
                    for j in range(TJ):
                        if ahead:
                            score(*ahead[j])
                        score_t(p, hd, j)
                    if ahead:
                        score(*ahead[3])
                    if half >= 1:
                        weigh(half - 1, hd % 4)
                    if hd == 2 and p + 2 < PAIRS:
                        proj(p + 2)
                    if hd == 3 and nxt:
                        max_rows(p + 1, 0)
                    if hd == 5 and p >= 1:
                        out_rows(p - 1)
                    if hd == 6 and nxt:
                        max_rows(p + 1, 1)
                    if hd in (5, 6) and p == PAIRS - 1:
                        transposes(PAIRS + hd - 5)
            for c in range(4):
                weigh(2 * PAIRS - 1, c)
            transposes(PAIRS + 2)

            def logits(t0, t1):
                pe.wait_ge(hnT_done, PAIRS + (t1 - 1) // TJ + 1)
                for t in range(t0, t1):
                    ins = pe.matmul(bank[RANK_BANK][:, E * t:E * (t + 1)], hnT[:, 128 * t:128 * (t + 1)], W("gate"), start=True, stop=True)
                if t1 == T:
                    ins.then_inc(lg_mm, 1)

            def sh_hidden(k):
                tc, ic = divmod(k, IC)
                pe.wait_ge(hnT_done, PAIRS + (4 * tc + 3) // TJ + 1)
                if k >= 4:
                    pe.wait_ge(sh_act, k - 3)
                elif k < 2:
                    pe.wait_ge(exp_done, TJ * HEADS * PAIRS)
                else:
                    pe.wait_ge(out_read, TJ * PAIRS)
                pe.matmul(bank[SH_BANKS[k % 4]][:, :], W("sw1")[:, 128 * ic:128 * (ic + 1)], hnT[:, 512 * tc:512 * (tc + 1)], start=True, stop=True)\
                    .then_inc(sh_mm, 1)

            def sh_out(tc):
                pe.wait_ge(sh_act, IC * (tc + 1))
                if tc == 0:
                    pe.wait_ge(av_free[1], 2 * PAIRS)
                if tc >= 2:
                    pe.wait_ge(sh_add, tc - 1)
                for i in range(4):
                    for ic in range(IC):
                        ins = pe.matmul(bank[SY_BANKS[tc]][:, 128 * i:128 * (i + 1)], a_sh[:, tc % 2, ic, 128 * i:128 * (i + 1)],
                                        W("sw2")[:, D * ic:D * (ic + 1)], start=(ic == 0), stop=(ic == IC - 1))
                ins.then_inc(sh_y, 1)

            sh_hidden(0)
            sh_hidden(1)
            pe.wait_ge(av_free[0], 2 * PAIRS)
            logits(0, 9)
            out_rows(PAIRS - 1)
            for k in range(2, 8):
                sh_hidden(k)
            transposes(PAIRS + 3)
            logits(9, T)
            sh_out(0)
            pe.wait_ge(oh_done, 1)
            rank = bank[RANK_BANK][:, 128:128 + T * E]
            ohv = oh_b[:, :, :].rearrange("p t e -> p (t e)")
            pe.matmul(rank, tri_b[:, :], ohv, start=True, stop=False)
            for u in range(1, T):
                pe.matmul(rank[:, E * u:T * E], ones_b[:, :], ohv[:, 0:E * (T - u)], start=False, stop=(u == T - 1))
            pe.matmul(bank[RANK_BANK][:, 256:256 + T * E], ones_b[:, :], ohv, start=True, stop=True).then_inc(rank_mm, 1)
            for k in range(8, 12):
                sh_hidden(k)
            sh_out(1)
            sh_out(2)

            def turn_x(t):
                pe.wait_ge(xs_ld[t % NX], 16 * (t // NX + 1))
                if t >= 1:
                    pe.wait_ge(x_cp, t)
                else:
                    pe.wait_ge(slot_done, 1)
                pe.transpose(bank[XT_BANK][:, 0:D], xs[:, t % NX, 0:D], ident).then_inc(x_tr, 1)

            def up(t, e, m):
                pe.wait_ge(x_cp, t + 1)
                if m == 0 and t >= 2:
                    pe.wait_ge(silu_done, t - 1)
                if m == 1 and t >= 2:
                    pe.wait_ge(gated, t - 1)
                pe.matmul(bank[UP_BANKS[m][t % 2]][:, :], xsT[:, t % 2, :], w13_sb[:, bass.ds(e, 1), m, :].rearrange("p a i -> p (a i)"), start=True, stop=True)\
                    .then_inc(up_b if m else up_a, 1)

            def turn_g(t):
                pe.wait_ge(gated, t + 1)
                if t >= 1:
                    pe.wait_ge(g_cp, t)
                for c in range(IC):
                    ins = pe.transpose(bank[GT_BANK][:, 128 * c:128 * (c + 1)], gate_sb[:, t % 2, 128 * c:128 * (c + 1)], ident)
                ins.then_inc(g_tr, 1)

            def down(t, e):
                pe.wait_ge(g_cp, t + 1)
                if t >= 2:
                    pe.wait_ge(y_cp, t - 1)
                elif t == 0:
                    pe.wait_ge(sh_add, 3)
                for c in range(IC):
                    ins = pe.matmul(bank[Y_BANKS[t % 2]][:, 0:D], gT[:, t % 2, 128 * c:128 * (c + 1)],
                                    w2_sb[:, bass.ds(e, 1), c, :].rearrange("p a d -> p (a d)"), start=(c == 0), stop=(c == IC - 1))
                ins.then_inc(y_mm, 1)

            def expert_of(t):
                return pe.value_load(et_i[0:1, t:t + 1], min_val=0, max_val=E - 1)

            pe.wait_ge(ld_exp, 16 * 2 * E)
            pe.wait_ge(et_done, 1)
            pe.wait_ge(sh_act, 3 * IC)
            turn_x(0)
            e, prev = expert_of(0), None
            for t in range(SLOT_TILES):
                up(t, e, 0)
                if t >= 1:
                    turn_g(t - 1)
                up(t, e, 1)
                nxt = expert_of(t + 1) if t + 1 < SLOT_TILES else None
                if t + 1 < SLOT_TILES:
                    turn_x(t + 1)
                if t >= 1:
                    down(t - 1, prev)
                e, prev = nxt, e
            turn_g(SLOT_TILES - 1)
            down(SLOT_TILES - 1, prev)


def layouts(inputs):
    a = {k: np.ascontiguousarray(v) for k, v in inputs.items()}
    g = lambda n: a["L0_" + n]
    f32 = np.float32
    x = a["x"].reshape(B, SIDE, PATCH, SIDE, PATCH).transpose(2, 4, 0, 1, 3).reshape(KC, 128, B * N_IMG).transpose(1, 0, 2)
    wn = np.stack([g("tok_" + n).T.reshape(KC, 128, 128).transpose(1, 0, 2) for n in ("W1_w", "W1_sw", "W2_w", "W2_sw")], axis=1)

    def heads(w):
        return w.reshape(-1, 2, HSC, DH).transpose(0, 1, 3, 2).reshape(-1, 2 * D)

    col = lambda v: v.reshape(-1, 128).T
    n = dict(ei1=col(g("tok_eps_in1")), ei2=col(g("tok_eps_in2")), eo1=col(g("tok_eps_out1")), eo2=col(g("tok_eps_out2")),
             b1=col(g("tok_W1_b")), sb1=col(g("tok_W1_sb")), b2=col(g("tok_W2_b")), sb2=col(g("tok_W2_sb")),
             bq=col(heads(g("attn_bq"))), bk=col(heads(g("attn_bk"))))
    npack = np.concatenate([n[k] for k in N_COLS], axis=1)
    rows = np.stack([g("tok_W3_b"), g("attn_bv")])[None]
    w = dict(wq=heads(g("attn_Wq")), wk=heads(g("attn_Wk")), wv=g("attn_Wv"), w3=g("tok_W3_w").T, sw1=g("ffn_sw1").T,
             sw2=g("ffn_sw2").T.reshape(IC, 128, D).transpose(1, 0, 2).reshape(128, IC * D), gate=g("ffn_gate_w").T)
    wpack = np.concatenate([w[k] for k in W_COLS], axis=1)
    w13 = np.stack([g("ffn_w1").transpose(0, 2, 1), g("ffn_w3").transpose(0, 2, 1)], axis=2)
    w2 = g("ffn_w2").transpose(0, 2, 1).reshape(E, IC, 128, D).transpose(0, 2, 1, 3)
    pos = np.arange(N_IMG, dtype=f32)[:, None]
    div = np.exp(np.arange(0, D, 2, dtype=f32) * f32(-math.log(10000.0) / D))
    ang = pos * div
    pe = np.stack([np.sin(ang), np.cos(ang)], axis=-1).reshape(N_IMG, D).astype(f32)
    c = dict(token=np.arange(B * SEQ, dtype=f32).reshape(T, 128).T, ident=np.eye(128, dtype=f32), tri=np.triu(np.ones((128, 128), f32), 1), ones=np.ones((128, 128), f32),
             pe=np.concatenate([pe, pe]), tile_no=np.tile(np.arange(SLOT_TILES, dtype=f32), (128, 1)),
             prio=np.tile(np.arange(E, 0, -1).astype(f32), (128, 1)))
    cpack = np.concatenate([c[k] for k in C_COLS], axis=1)
    return {k: np.ascontiguousarray(v) for k, v in dict(xT=x, txt=a["txt"], wn=wn, npack=npack, rows=rows, wpack=wpack,
                                                        cpack=cpack, w13=w13, w2=w2).items()}


def kernel(**inputs):
    import concourse.bacc as bacc
    from concourse.bass_utils import run_bass_kernel_spmd

    nc = bacc.Bacc("TRN2", target_bir_lowering=False, num_devices=1)
    arrays, args = {}, []
    for name, a in layouts(inputs).items():
        arrays[f"in_{name}_dram"] = a
        args.append(nc.dram_tensor(f"in_{name}_dram", a.shape, mybir.dt.from_np(a.dtype), kind="ExternalInput").ap())
    o = nc.dram_tensor("out_dram", (B * SEQ, D), mybir.dt.float32, kind="ExternalOutput").ap()
    build_kernel(nc, *args, o)
    r = run_bass_kernel_spmd(nc, [arrays], core_ids=[0])
    return r.results[0]["out_dram"].reshape(B, SEQ, D)
```

```python
import math

import numpy as np

import concourse.bass as bass
from concourse import mybir
from contextlib import ExitStack

B, IMG_SIDE, PATCH = 8, 128, 16
SIDE = IMG_SIDE // PATCH
N_IMG, N_TXT = SIDE * SIDE, 128
SEQ = N_IMG + N_TXT
D = 128
T = B * SEQ // 128
PAIRS = B // 2
TJ = 3
PT = TJ * 128
HEADS, DH = 8, 16
HS = 2 * HEADS
HSC = 8
LAM = 0.5
KC = PATCH * PATCH // 128
E, I = 8, 512
IC = I // 128
SLOT_TILES = (B * SEQ + E * 127) // 128
EPS = 1e-5
NPART = 3
K_PARTS = (0, 1, 2, 0, 1, 0)
Q_PARTS = (0, 0, 0, 1, 1, 2)
SROWS = 16 * len(K_PARTS)
SHALF = SEQ - 128

W_COLS = dict(wq=2 * D, wk=2 * D, wv=D, w3=D, sw1=I, sw2=IC * D, gate=E)
C_COLS = dict(ident=128, tri=128, ones=128, pe=128, tile_no=SLOT_TILES, prio=E, token=T)
XW = D + 1
NO_TOKEN = 4096.0
HALF_TOK = B * N_IMG // 2
N_COLS = dict(ei1=KC, ei2=KC, eo1=1, eo2=1, b1=1, sb1=1, b2=1, sb2=1, bq=2, bk=2)


def columns(cols):
    at, out = 0, {}
    for name, n in cols.items():
        out[name] = slice(at, at + n)
        at += n
    return out, at


def build_kernel(nc, xT, txt, wn, npack, rows, wpack, cpack, w13, w2, out):
    F32, BF16 = mybir.dt.float32, mybir.dt.bfloat16
    I32, U32 = mybir.dt.int32, mybir.dt.uint32
    ALU, ACT, AX = mybir.AluOpType, mybir.ActivationFunctionType, mybir.AxisListType
    WC, WN = columns(W_COLS)
    CC, CN = columns(C_COLS)
    NC_, NN = columns(N_COLS)

    split_dram = nc.dram_tensor("split_scratch", [4 * PAIRS, NPART, 128, PT], BF16, kind="Internal").ap()
    xs_dram = nc.dram_tensor("xs_scratch", [SLOT_TILES * 128, XW], F32, kind="Internal").ap()
    base_dram = nc.dram_tensor("base_scratch", [B * SEQ, D], F32, kind="Internal").ap()

    ctx = ExitStack()
    with ctx:
        def sb(name, shape, dt=F32):
            return ctx.enter_context(nc.sbuf_tensor(name, shape, dt))

        def sem(name):
            return ctx.enter_context(nc.semaphore(name))

        bank = [ctx.enter_context(nc.psum_tensor(f"bank{i}", [128, 512], F32)) for i in range(8)]

        NST = 3
        SF = HS * PT // 2
        stacks = sb("stacks", [128, 2 * NST * 2 * SF], BF16)
        words = stacks[:, :].bitcast(F32)
        free_q = words[:, 4 * SF:5 * SF]
        free_k = words[:, 5 * SF:6 * SF]
        assert E * (2 * I + IC * D) <= 4 * SF
        w13_sb = words[:, 2 * SF:2 * SF + E * 2 * I].rearrange("p (e m i) -> p e m i", e=E, m=2)
        w2_sb = words[:, 2 * SF + E * 2 * I:2 * SF + E * (2 * I + IC * D)].rearrange("p (e c d) -> p e c d", e=E, c=IC)
        x_sb = free_k[:, 0:1024].rearrange("p (c t) -> p c t", c=KC)
        wn_sb = free_k[:, 1024:2048].rearrange("p (m c n) -> p m c n", m=4, c=KC)
        np_sb = sb("np_sb", [128, NN])
        rows_sb = sb("rows_sb", [128, 2, 128])
        wp_sb = sb("wp_sb", [128, WN])
        c_sb = sb("c_sb", [128, CN])

        def W(name):
            return wp_sb[:, WC[name]]

        def C(name):
            return c_sb[:, CC[name]]

        def N(name):
            return np_sb[:, NC_[name]]

        ident = C("ident")

        noise = sb("noise", [128, 6])
        nz_abs, nz_y, nz_u = [sb(f"nz{i}", [128, 6]) for i in range(3)]
        diag = sb("diag", [128, 2, 128])
        wt = free_k[:, 2048:2304].rearrange("p (c n) -> p c n", c=KC)
        w1n = free_k[:, 2304:2560].rearrange("p (c n) -> p c n", c=KC)
        w2n = free_k[:, 2560:2816].rearrange("p (c n) -> p c n", c=KC)
        bn_ = sb("bn_", [128, 2])
        bq4 = sb("bq4", [128, 2])
        peb = sb("peb", [128, 128])
        g_sb = free_q[:, 0:512]
        inner = free_q[:, 512:1024]
        gm = free_q[:, 1024:1536]
        ex = free_q[:, 1536:2048]
        mu = free_q[:, 2048:2560]
        mr = free_q[:, 2560:3072]

        h = sb("h", [128, T, D])
        hn = sb("hn", [128, T, XW])
        hnT = sb("hnT", [128, T * 128])
        stats = sb("stats", [128, T, 6])
        mv = sb("mv", [128, T, 2])
        ve = sb("ve", [128, T])
        rstd = sb("rstd", [128, T])
        ln_u = sb("ln_u", [128, T])

        NF = 4
        f_ring = sb("f_ring", [128, NF, PT])
        r1, r1v = sb("r1", [128, PT]), sb("r1v", [128, PT])
        parts = sb("parts", [128, NF, NPART, PT], BF16)
        q_st, k_st = [[stacks[:, (2 * i + m) * 2 * SF:(2 * i + m + 1) * 2 * SF].rearrange("p (g t) -> p g t", g=HS) for i in range(NST)] for m in range(2)]
        vaug = sb("vaug", [128, T, HEADS, 32])
        smax = sb("smax", [128, 2, TJ, HS])
        mx_r = sb("mx_r", [128, TJ, HSC])
        mx_s = sb("mx_s", [128, 2, TJ, NPART, HSC], BF16)
        mx_p = sb("mx_p", [NPART * HSC, 2, PT], BF16)
        GH = TJ * HEADS // 2
        p_ring = sb("p_ring", [128, 2, GH, 2, SEQ])
        oT = sb("oT", [128, 2, 2, PT])
        rs = sb("rs", [128, TJ, HS])
        o1 = sb("o1", [128, TJ, HS, DH])
        o2 = sb("o2", [128, TJ * D])

        lg = sb("lg", [128, T, E])
        mxl = sb("mxl", [128, T])
        oh = sb("oh", [128, T, E])
        oh_b = sb("oh_b", [128, T, E], BF16)
        tri_b = sb("tri_b", [128, 128], BF16)
        ones_b = sb("ones_b", [128, 128], BF16)
        ident_b = sb("ident_b", [128, 128], BF16)
        cnt = sb("cnt", [128, E])
        cnt_i = sb("cnt_i", [128, E], I32)
        tiles_e = sb("tiles_e", [128, E])
        incl = sb("incl", [128, E])
        base = sb("base", [128, E])
        one8 = sb("one8", [128, E])
        slot_f = sb("slot_f", [128, T])
        slot_u = sb("slot_u", [128, T], U32)
        cmp = sb("cmp", [128, SLOT_TILES, E])
        et_f = sb("et_f", [128, SLOT_TILES])
        et_i = sb("et_i", [128, SLOT_TILES], I32)
        empty = sb("empty", [128, XW])
        spaces = {"stack": [words, 0], "exp": [p_ring[:, :, :, :, :].rearrange("p a g s q -> p (a g s q)"), 0]}

        def carve(where, *shape):
            space, at = spaces[where]
            n = math.prod(shape)
            spaces[where][1] += n
            v = space[:, at:at + n]
            names = "abc"[:len(shape)]
            return v.rearrange(f"p ({' '.join(names)}) -> p {' '.join(names)}", **dict(zip(names, shape)))

        a_sh = carve("stack", 2, IC, 512)
        NX = 3
        xs = carve("exp", NX, XW)
        xsT = carve("exp", 2, D)
        sA = carve("stack", 2, I)
        gate_sb = carve("stack", 2, I)
        gT = carve("exp", 2, I)
        NY = 3
        y_sb = carve("exp", NY, D)
        y_base = carve("exp", NY, D)
        id_u = sb("id_u", [128, SLOT_TILES], U32)
        assert spaces["stack"][1] <= 2 * SF

        ld_x, ld_wn, ld_rows, ld_wp, ld_c, ld_txt, ld_np = [sem(f"ld_{n}") for n in ("x", "wn", "rows", "wp", "c", "txt", "np")]
        ld_exp = sem("ld_exp")
        dve_step, pool_step = sem("dve_step"), sem("pool_step")
        diag_done, eo_mm = sem("diag_done"), sem("eo_mm")
        noisy = sem("noisy")
        tok_mm = sem("tok_mm")
        gm_done = sem("gm_done")
        ex_done = sem("ex_done")
        act_done = sem("act_done")
        h_mm = sem("h_mm")
        hn_ready = sem("hn_ready")
        tr_done = sem("tr_done")
        hnT_done = sem("hnT_done")
        bq_done = sem("bq_done")
        misc_ready = sem("misc_ready")
        out_read = sem("out_read")
        f_done = sem("f_done")
        hi_done = sem("hi_done")
        split_done = [sem(f"split_done{i}") for i in range(NF)]
        split_wr = [sem(f"split_wr{i}") for i in range(NF)]
        stack_ld = [[sem(f"stack_ld{i}{c}") for c in range(2)] for i in range(NST)]
        max_ld = [[sem(f"max_ld{i}{c}") for c in range(2)] for i in range(NST)]
        init_done = sem("init_done")
        ones_done = sem("ones_done")
        v_done = sem("v_done")
        s_ready, s_max = sem("s_ready"), sem("s_max")
        mx_evac, mx_split = sem("mx_evac"), sem("mx_split")
        st_ready, exp_done = sem("st_ready"), sem("exp_done")
        av_done, av_free = sem("av_done"), [sem("av_free0"), sem("av_free1")]
        lg_mm, oh_done, rank_mm, slot_done, et_done = [sem(n) for n in ("lg_mm", "oh_done", "rank_mm", "slot_done", "et_done")]
        zero_done, xs_zeroed, scattered = sem("zero_done"), sem("xs_zeroed"), sem("scattered")
        sh_mm, sh_act, sh_y, sh_add = [sem(n) for n in ("sh_mm", "sh_act", "sh_y", "sh_add")]
        xs_ld = [sem(f"xs_ld{i}") for i in range(NX)]
        x_tr, x_cp, up_a, up_b, silu_done, gated, g_tr, g_cp, y_mm, y_cp = [sem(n) for n in (
            "x_tr", "x_cp", "up_a", "up_b", "silu_done", "gated", "g_tr", "g_cp", "y_mm", "y_cp")]
        id_done, base_clear, base_st = sem("id_done"), sem("base_clear"), sem("base_st")
        based = [sem(f"based{i}") for i in range(NY)]
        stored = [sem(f"stored{i}") for i in range(NY)]

        INIT = 6

        def proj_items(p):
            return [("proj", p, n) for n in range(5)]

        misc_order = proj_items(0) + proj_items(1) + [("max", 0, 0), ("max", 0, 1)]
        for p in range(PAIRS):
            misc_order += proj_items(p + 2) if p + 2 < PAIRS else []
            misc_order += [("max", p + 1, 0)] if p + 1 < PAIRS else []
            misc_order += [("out", p - 1, 0)] if p >= 1 else []
            misc_order += [("max", p + 1, 1)] if p + 1 < PAIRS else []
            misc_order += [("out", p - 1, j) for j in range(1, TJ)] if p >= 1 else []
        misc_order += [("out", PAIRS - 1, j) for j in range(TJ)]
        misc_no = {item: n for n, item in enumerate(misc_order)}

        SH_BANKS, SY_BANKS = (2, 3, 6, 7), (5, 0, 5)
        UP_BANKS, GT_BANK, XT_BANK, Y_BANKS, RANK_BANK = ((2, 3), (6, 7)), 1, 4, (5, 0), 4

        def mbank(item):
            return bank[6 + misc_no[item] % 2]

        def evacuated(item):
            kind, p, n = item
            if kind == "proj":
                return (f_done, 4 * p + n + 1) if n < 4 else (v_done, p + 1)
            return (mx_evac, 2 * p + n + 1) if kind == "max" else (out_read, TJ * p + n + 1)

        def batches(j):
            return {0: [(0, 128, 0)], 1: [(0, SHALF, 0), (SHALF, 128 - SHALF, 1)], 2: [(0, 128, 1)]}[j]

        block = ctx.enter_context(nc.Block())

        @block.sync
        def _(sp):
            sp.dma_start(np_sb[:, :], npack).then_inc(ld_np, 16)
            sp.dma_start(c_sb[:, :], cpack).then_inc(ld_c, 16)
            sp.dma_start(wn_sb, wn).then_inc(ld_wn, 16)
            sp.dma_start(x_sb, xT).then_inc(ld_x, 16)
            sp.dma_start(rows_sb[:, :, :], rows.to_broadcast([128, 2, 128])).then_inc(ld_rows, 16)
            sp.dma_start(wp_sb[:, :], wpack).then_inc(ld_wp, 16)
            for b in range(B):
                p, odd = divmod(b, 2)
                if odd:
                    sp.dma_start(h[:, TJ * p + 2, :], txt[b, :, :]).then_inc(ld_txt, 16)
                else:
                    sp.dma_start(h[N_IMG:128, TJ * p, :], txt[b, 0:128 - N_IMG, :]).then_inc(ld_txt, 16)
                    sp.dma_start(h[0:SHALF, TJ * p + 1, :], txt[b, 128 - N_IMG:128, :]).then_inc(ld_txt, 16)

            def store_parts(r):
                sp.wait_ge(split_done[r % NF], r // NF + 1)
                sp.dma_start(split_dram[r, :, :, :].rearrange("s x t -> x s t"), parts[:, r % NF, :, :])\
                    .then_inc(split_wr[r % NF], 16)

            def load_stacks(p, ch):
                b = p % NST
                if p >= NST:
                    sp.wait_ge(st_ready, TJ * HEADS * (p - NST + 1))
                for m, st, blocks in ((0, q_st[b], ((0, 3, 0, 1), (3, 2, 1, 1), (5, 1, 2, 1))), (1, k_st[b], ((0, 1, 0, 3), (3, 1, 0, 2), (5, 1, 0, 1)))):
                    r = 4 * p + 2 * ch + m
                    sp.wait_ge(split_wr[r % NF], 16 * (r // NF + 1))
                    src = split_dram[r, :, :, :].rearrange("s (d g) t -> s d (g t)", g=HSC)
                    for j, copies, s, n in blocks:
                        dst = st[16 * j:16 * (j + copies * n), HSC * ch:HSC * (ch + 1), :].rearrange("p g t -> p (g t)")
                        part = src[s:s + 1, :, :].to_broadcast([copies, 16, HSC * PT]) if m == 0 else \
                            src[s:s + n, :, :].rearrange("s d x -> (s d) x")
                        sp.dma_start(dst, part).then_inc(stack_ld[b][ch], 16)

            def load_max(p, ch):
                b = p % NST
                sp.wait_ge(mx_evac, 2 * p + ch + 1)
                for s in range(NPART):
                    sp.dma_start(q_st[b][SROWS + s:SROWS + s + 1, HSC * ch:HSC * (ch + 1), :], mx_p[HSC * s:HSC * (s + 1), ch, :])\
                        .then_inc(max_ld[b][ch], 16)

            def send(p, ch):
                for n in (2 * ch, 2 * ch + 1):
                    store_parts(4 * p + n)
                load_stacks(p, ch)

            for n in range(4):
                store_parts(n)
            for ch in range(2):
                load_stacks(0, ch)
            for ch in range(2):
                send(1, ch)
                load_max(0, ch)
            sp.wait_ge(zero_done, 1)
            for t in range(SLOT_TILES):
                sp.dma_start(xs_dram[128 * t:128 * (t + 1), :], empty[:, :]).then_inc(xs_zeroed, 16)
            for p in range(1, PAIRS):
                for ch in range(2):
                    if p + 1 < PAIRS:
                        send(p + 1, ch)
                    load_max(p, ch)
            sp.wait_ge(st_ready, TJ * HEADS * (PAIRS - 1))
            for e in range(E):
                sp.dma_start(w13_sb[:, e, :, :], w13[e, :, :, :]).then_inc(ld_exp, 16)
                sp.dma_start(w2_sb[:, e, :, :], w2[e, :, :, :]).then_inc(ld_exp, 16)

            def load_xs(t):
                if t >= NX:
                    sp.wait_ge(x_tr, t - NX + 1)
                    sp.wait_ge(id_done, t - NX + 1)
                sp.dma_start(xs[:, t % NX, :], xs_dram[128 * t:128 * (t + 1), :]).then_inc(xs_ld[t % NX], 16)

            base_v = base_dram.rearrange("(t p) d -> p t d", p=128)
            for tc in range(2):
                sp.wait_ge(sh_add, tc + 1)
                sp.dma_start(base_v[:, 4 * tc:4 * tc + 4, :], h[:, 4 * tc:4 * tc + 4, :]).then_inc(base_st, 16)
            sp.wait_ge(scattered, 16 * T)
            for t in range(NX):
                load_xs(t)
            sp.wait_ge(sh_add, 3)
            sp.dma_start(base_v[:, 8:12, :], h[:, 8:12, :]).then_inc(base_st, 16)
            for t in range(NX, SLOT_TILES):
                load_xs(t)

        @block.gpsimd
        def _(pool):
            steps = [0]

            def link(ins):
                steps[0] += 1
                ins.then_inc(pool_step, 1)
                pool.wait_ge(pool_step, steps[0])

            link(pool.memset(empty[:, 0:D], 0.0))
            pool.memset(empty[:, D:XW], NO_TOKEN).then_inc(zero_done, 1)
            pool.wait_ge(zero_done, 1)

            def ones_rows(b):
                if b == NST - 1:
                    pool.wait_ge(h_mm, 2)
                pool.memset(k_st[b][SROWS:SROWS + NPART, :, :], 1.0).then_inc(ones_done, 1)
                pool.wait_ge(ones_done, b + 1)

            def split(r):
                pool.wait_ge(f_done, r + 1)
                pool.wait_ge(hi_done, r + 1)
                f, pr = f_ring[:, r % NF, :], parts[:, r % NF, :, :]
                link(pool.tensor_tensor(r1[:, :], f, pr[:, 0, :], ALU.subtract))
                link(pool.tensor_scalar(pr[:, 1, :], r1[:, :], 1.0, 0.0, ALU.mult, ALU.add))
                pool.tensor_tensor(pr[:, 2, :], r1[:, :], pr[:, 1, :], ALU.subtract).then_inc(split_done[r % NF], 1)
                pool.wait_ge(split_done[r % NF], r // NF + 1)

            ones_rows(0)
            ones_rows(1)
            pool.memset(vaug[:, :, :, DH:DH + 1], 1.0).then_inc(init_done, 1)
            pool.memset(vaug[:, :, :, DH + 1:32], 0.0).then_inc(init_done, 1)
            pool.memset(one8[:, :], 1.0).then_inc(init_done, 1)
            pool.wait_ge(ld_c, 16)
            for dst, name in ((ident_b, "ident"), (tri_b, "tri"), (ones_b, "ones")):
                pool.tensor_copy(dst[:, :], C(name)).then_inc(init_done, 1)
            pool.wait_ge(init_done, INIT)
            for r in range(4 * PAIRS):
                if r in (1, 3):
                    continue
                split(r)
                if r == 7:
                    ones_rows(2)

            pool.wait_ge(slot_done, 1)
            pool.wait_ge(xs_zeroed, 16 * SLOT_TILES)
            for t in range(T):
                pool.indirect_dma_start(out=xs_dram, out_offset=bass.IndirectOffsetOnAxis(ap=slot_u[:, t:t + 1], axis=0),
                                        in_=hn[:, t, :], in_offset=None).then_inc(scattered, 16)

            def index(t):
                return bass.IndirectOffsetOnAxis(ap=id_u[:, t:t + 1], axis=0)

            def gather_base(t):
                pool.wait_ge(id_done, t + 1)
                if t == 0:
                    pool.wait_ge(base_st, 16 * 3)
                    pool.wait_ge(base_clear, 1)
                if t >= NY:
                    pool.wait_ge(y_cp, t - NY + 1)
                pool.indirect_dma_start(out=y_base[:, t % NY, :], out_offset=None, in_=base_dram, in_offset=index(t),
                                        bounds_check=B * SEQ - 1, oob_is_err=False).then_inc(based[t % NY], 16)

            gather_base(0)
            gather_base(1)
            for t in range(SLOT_TILES):
                pool.wait_ge(y_cp, t + 1)
                pool.indirect_dma_start(out=out, out_offset=index(t), in_=y_sb[:, t % NY, :], in_offset=None,
                                        bounds_check=B * SEQ - 1, oob_is_err=False).then_inc(stored[t % NY], 16)
                if t + 2 < SLOT_TILES:
                    gather_base(t + 2)
            for i in range(NY):
                pool.wait_ge(stored[i], 16 * len(range(i, SLOT_TILES, NY)))

        @block.scalar
        def _(act):
            for half in range(2):
                act.wait_ge(gm_done, half + 1)
                c = slice(HALF_TOK * half, HALF_TOK * (half + 1))
                act.activation(ex[:, c], gm[:, c], ACT.Exp).then_inc(ex_done, 1)

            def copy_hnT(n):
                act.wait_ge(tr_done, n + 1)
                c = PT * (n % PAIRS)
                act.activation(hnT[:, c:c + PT], bank[n % 2][:, 0:PT], ACT.Copy).then_inc(hnT_done, 1)

            def evac_proj(p, n):
                r = 4 * p + n
                item = ("proj", p, n)
                act.wait_ge(misc_ready, misc_no[item] + 1)
                if r >= NF:
                    act.wait_ge(split_done[r % NF], r // NF)
                    act.wait_ge(split_wr[r % NF], 16 * (r // NF))
                bias = N("bk")[:, n // 2:n // 2 + 1] if n % 2 else bq4[:, n // 2:n // 2 + 1]
                for dst, done in ((parts[:, r % NF, 0, :], hi_done), (f_ring[:, r % NF, :], f_done)):
                    act.activation(dst, mbank(item)[:, 0:PT], ACT.Identity, bias=bias, scale=1.0 if n % 2 else DH ** -0.5).then_inc(done, 1)

            def evac_max(p, ch):
                item = ("max", p, ch)
                act.wait_ge(misc_ready, misc_no[item] + 1)
                if p >= 1:
                    act.wait_ge(max_ld[(p - 1) % NST][ch], 16 * NPART * ((p - 1) // NST + 1))
                act.activation(mx_p[:, ch, :], mbank(item)[0:NPART * HSC, 0:PT], ACT.Copy).then_inc(mx_evac, 1)

            def exp(p, hd, j):
                g = TJ * (HEADS * p + hd) + j
                act.wait_ge(st_ready, g + 1)
                half = g // GH
                if half >= 2:
                    act.wait_ge(av_done, 4 * (half - 1))
                act.activation(p_ring[:, half % 2, g % GH, :, :], bank[2 + g % 2][:, 0:2 * SEQ].rearrange("p (s q) -> p s q", s=2),
                               ACT.Exp).then_inc(exp_done, 1)

            def evac_av(half, bb):
                act.wait_ge(av_done, 4 * half + 2 * (bb + 1))
                if half >= 2 and half % 2 == 0 and bb == 0:
                    act.wait_ge(misc_ready, misc_no[("out", half // 2 - 1, TJ - 1)] + 1)
                act.activation(oT[:, half % 2, :, SEQ * bb:SEQ * (bb + 1)],
                               bank[4 + bb][:, 0:2 * SEQ].rearrange("p (s q) -> p s q", s=2), ACT.Copy).then_inc(av_free[bb], 1)

            copy_hnT(0)
            act.wait_ge(bq_done, 1)
            for n in range(4):
                evac_proj(0, n)
            copy_hnT(1)
            for n in range(4):
                evac_proj(1, n)
            copy_hnT(2)
            copy_hnT(3)
            evac_max(0, 0)
            for p in range(PAIRS):
                for hd in range(HEADS):
                    half = 2 * p + hd // 4
                    exp(p, hd, 0)
                    if (p, hd) == (0, 0):
                        evac_max(0, 1)
                    if hd in (1, 2) and p + 2 < PAIRS:
                        evac_proj(p + 2, 2 * hd - 1)
                    exp(p, hd, 1)
                    if hd == 6 and p + 1 < PAIRS:
                        evac_max(p + 1, 1)
                    exp(p, hd, 2)
                    if hd in (0, 1) and p + 2 < PAIRS:
                        evac_proj(p + 2, 2 * hd)
                    if hd % 4 == 0 and half >= 2:
                        evac_av(half - 2, 1)
                    if hd == 3 and p + 1 < PAIRS:
                        evac_max(p + 1, 0)
                    if hd in (2, 7) and half >= 1:
                        evac_av(half - 1, 0)
                    if hd in (3, 4) and p == PAIRS - 1:
                        copy_hnT(PAIRS + hd - 3)
            evac_av(2 * PAIRS - 2, 1)
            evac_av(2 * PAIRS - 1, 0)
            evac_av(2 * PAIRS - 1, 1)
            copy_hnT(PAIRS + 2)

            def gelu(k):
                act.wait_ge(sh_mm, k + 1)
                tc, ic = divmod(k, IC)
                if tc >= 2:
                    act.wait_ge(sh_y, tc - 1)
                act.activation(a_sh[:, tc % 2, ic, :], bank[SH_BANKS[k % 4]][:, :], ACT.Gelu).then_inc(sh_act, 1)

            for k in range(4):
                gelu(k)
            copy_hnT(PAIRS + 3)
            for k in range(4, 3 * IC):
                gelu(k)

            def silu(t):
                act.wait_ge(up_a, t + 1)
                if t >= 2:
                    act.wait_ge(gated, t - 1)
                act.activation(sA[:, t % 2, :], bank[UP_BANKS[0][t % 2]][:, :], ACT.Silu).then_inc(silu_done, 1)

            def copy_gT(t):
                act.wait_ge(g_tr, t + 1)
                if t >= 2:
                    act.wait_ge(y_mm, t - 1)
                act.activation(gT[:, t % 2, :], bank[GT_BANK][:, :], ACT.Copy).then_inc(g_cp, 1)

            for t in range(SLOT_TILES):
                silu(t)
                if t >= 1:
                    copy_gT(t - 1)
            copy_gT(SLOT_TILES - 1)

        @block.vector
        def _(dve):
            steps = [0]

            def link(ins):
                steps[0] += 1
                ins.then_inc(dve_step, 1)
                dve.wait_ge(dve_step, steps[0])

            def rsqrt(y, v, u):
                vi, yi = v.bitcast(U32), y.bitcast(I32)
                link(dve.tensor_scalar(y.bitcast(U32), vi, 1, None, ALU.logical_shift_right))
                link(dve.tensor_scalar(yi, yi, -1.0, float(0x5F3759DF), ALU.mult, ALU.add))
                for _ in range(3):
                    link(dve.tensor_tensor(u, v, y, ALU.mult))
                    link(dve.scalar_tensor_tensor(u, u, -0.5, y, ALU.mult, ALU.mult))
                    link(dve.scalar_tensor_tensor(y, u, 1.5, y, ALU.add, ALU.mult))

            dve.wait_ge(ld_np, 16)
            eps = np_sb[:, 0:6]
            link(dve.tensor_scalar(nz_abs[:, :].bitcast(U32), eps.bitcast(U32), 0x7FFFFFFF, None, ALU.bitwise_and))
            rsqrt(nz_y[:, :], nz_abs[:, :], nz_u[:, :])
            link(dve.tensor_tensor(noise[:, :], eps, nz_y[:, :], ALU.mult))
            dve.wait_ge(ld_c, 16)
            for m in range(2):
                dve.tensor_scalar(diag[:, m, :], ident, noise[:, 4 + m:5 + m], None, ALU.mult).then_inc(diag_done, 1)
            dve.wait_ge(ld_wn, 16)
            dve.wait_ge(eo_mm, 1)
            for m, wdst in enumerate((w1n, w2n)):
                for kc in range(KC):
                    ins = dve.scalar_tensor_tensor(wt[:, kc, :], bank[6][:, 128 * m:128 * (m + 1)], noise[:, 2 * m + kc:2 * m + kc + 1],
                                                   wn_sb[:, 2 * m + 1, kc, :], ALU.mult, ALU.mult)
                link(ins)
                dve.tensor_tensor(wdst[:, :, :], wt[:, :, :], wn_sb[:, 2 * m, :, :], ALU.add).then_inc(noisy, 1)
                dve.wait_ge(noisy, m + 1)
            for m, (bb, ss) in enumerate((("b1", "sb1"), ("b2", "sb2"))):
                ins = dve.scalar_tensor_tensor(bn_[:, m:m + 1], N(ss), noise[:, 4 + m:5 + m], N(bb), ALU.mult, ALU.add)
            ins.then_inc(noisy, 1)
            dve.tensor_scalar(bq4[:, :], N("bq"), DH ** -0.5, None, ALU.mult).then_inc(bq_done, 1)
            dve.wait_ge(ld_rows, 16)
            link(dve.tensor_tensor(peb[:, :], C("pe"), rows_sb[:, 0, :], ALU.add))
            dve.tensor_copy(hn[:, :, D], C("token"))

            dve.wait_ge(noisy, 3)
            for half in range(2):
                c = slice(HALF_TOK * half, HALF_TOK * (half + 1))
                dve.wait_ge(tok_mm, 2 * half + 1)
                dve.tensor_scalar(gm[:, c], bank[3 * half][:, 0:HALF_TOK], bn_[:, 0:1], 20.0, ALU.add, ALU.min).then_inc(gm_done, 1)

            def mish(half):
                c = slice(HALF_TOK * half, HALF_TOK * (half + 1))
                dve.wait_ge(tok_mm, 2 * half + 2)
                link(dve.tensor_scalar(inner[:, c], bank[3 * half + 1][:, 0:HALF_TOK], bn_[:, 1:2], None, ALU.add))
                dve.wait_ge(ex_done, half + 1)
                link(dve.scalar_tensor_tensor(mu[:, c], ex[:, c], 2.0, ex[:, c], ALU.add, ALU.mult))
                dve.scalar_tensor_tensor(inner[:, c], bank[3 * half][:, 0:HALF_TOK], bn_[:, 0:1], inner[:, c], ALU.add, ALU.mult)
                link(dve.tensor_scalar(mr[:, c], mu[:, c], 2.0, None, ALU.add))
                link(dve.reciprocal(ex[:, c], mr[:, c]))
                link(dve.tensor_tensor(mu[:, c], mu[:, c], ex[:, c], ALU.mult))
                dve.tensor_tensor(g_sb[:, c], mu[:, c], inner[:, c], ALU.mult).then_inc(act_done, 1)

            hv = h[:, :, :].rearrange("p (a j) d -> p a j d", j=TJ)

            def image_tokens(half):
                dve.wait_ge(h_mm, half + 1)
                n = PAIRS // 2
                for odd in range(2):
                    q = slice(64 * odd, 64 * odd + 64)
                    pb = peb[q, :].rearrange("p (a d) -> p a d", a=1).to_broadcast([64, n, D])
                    link(dve.tensor_tensor(hv[q, n * half:n * (half + 1), odd, :], bank[2 + 3 * half][q, 0:n * D].rearrange("p (a d) -> p a d", a=n), pb, ALU.add))

            def ln_stats(t0, t1):
                for t in range(t0, t1):
                    ins = dve.bn_stats(stats[:, t, :], h[:, t, :])
                link(ins)
                for t in range(t0, t1):
                    ins = dve.bn_aggr(mv[:, t, :], stats[:, t, :])
                link(ins)

            def ln_scale(t0, t1):
                link(dve.tensor_scalar(ve[:, t0:t1], mv[:, t0:t1, 1], EPS, None, ALU.add))
                rsqrt(rstd[:, t0:t1], ve[:, t0:t1], ln_u[:, t0:t1])
                for t in range(t0, t1):
                    dve.tensor_scalar(hn[:, t, 0:D], h[:, t, :], mv[:, t, 0:1], rstd[:, t:t + 1], ALU.subtract, ALU.mult)\
                        .then_inc(hn_ready, 1)

            def split(r):
                f, pr = f_ring[:, r % NF, :], parts[:, r % NF, :, :]
                dve.wait_ge(hi_done, r + 1)
                dve.wait_ge(f_done, r + 1)
                link(dve.tensor_tensor(r1v[:, :], f, pr[:, 0, :], ALU.subtract))
                link(dve.tensor_copy(pr[:, 1, :], r1v[:, :]))
                dve.tensor_tensor(pr[:, 2, :], r1v[:, :], pr[:, 1, :], ALU.subtract).then_inc(split_done[r % NF], 1)
                dve.wait_ge(split_done[r % NF], 1)

            def take_v(p):
                item = ("proj", p, 4)
                dve.wait_ge(misc_ready, misc_no[item] + 1)
                bv = rows_sb[:, 1:2, :].rearrange("p a (h d) -> p a h d", d=DH).to_broadcast([128, TJ, HEADS, DH])
                dve.tensor_tensor(vaug[:, TJ * p:TJ * (p + 1), :, 0:DH], mbank(item)[:, 0:PT].rearrange("p (j h d) -> p j h d", j=TJ, d=DH),
                                  bv, ALU.add).then_inc(v_done, 1)

            def row_max(p, hd, j):
                g = TJ * (HEADS * p + hd) + j
                dve.wait_ge(s_ready, g + 1)
                if p >= 2 and g % (TJ * HEADS) == 0:
                    dve.wait_ge(mx_split, 2 * (p - 1))
                dve.tensor_reduce(smax[:, p % 2, j, 2 * hd:2 * hd + 2], bank[g % 2][:, 0:2 * SEQ].rearrange("p (s k) -> p s k", s=2),
                                  AX.X, ALU.max, negate=True).then_inc(s_max, 1)

            def split_max(p, ch):
                dve.wait_ge(s_max, TJ * HEADS * p + GH * (ch + 1))
                if p >= 1:
                    dve.wait_ge(misc_ready, misc_no[("max", p - 1, ch)] + 1)
                if p + ch >= 1:
                    dve.wait_ge(mx_split, 2 * p + ch)
                src = smax[:, p % 2, :, HSC * ch:HSC * (ch + 1)]
                link(dve.tensor_copy(mx_s[:, ch, :, 0, :], src))
                link(dve.tensor_tensor(mx_r[:, :, :], src, mx_s[:, ch, :, 0, :], ALU.subtract))
                link(dve.tensor_copy(mx_s[:, ch, :, 1, :], mx_r[:, :, :]))
                dve.tensor_tensor(mx_s[:, ch, :, 2, :], mx_r[:, :, :], mx_s[:, ch, :, 1, :], ALU.subtract).then_inc(mx_split, 1)

            def out_tile(p, j):
                item = ("out", p, j)
                dve.wait_ge(misc_ready, misc_no[item] + 1)
                v = mbank(item)[:, :].rearrange("p (a c) -> p a c", c=32)
                link(dve.reciprocal(rs[:, j, :], v[:, :, DH]))
                rv = rs[:, j, :].rearrange("p (a s b) -> p a s b", s=2, b=4)
                link(dve.tensor_scalar(rv[:, :, 1, :], rv[:, :, 1, :], -LAM, None, ALU.mult))
                dve.tensor_tensor(o1[:, j, :, :], v[:, :, 0:DH], rs[:, j, :].rearrange("p (a c) -> p a c", c=1).to_broadcast([128, HS, DH]), ALU.mult)\
                    .then_inc(out_read, 1)

            def out_join(p):
                dve.wait_ge(out_read, TJ * (p + 1))
                ov = o1[:, :, :, :].rearrange("p j (a s b) d -> p (j a) s (b d)", s=2, b=4)
                hp = h[:, TJ * p:TJ * (p + 1), :].rearrange("p j (a x) -> p (j a) x", a=2)
                o2v = o2[:, :].rearrange("p (a x) -> p a x", a=2 * TJ)
                link(dve.tensor_tensor(o2v, ov[:, :, 0, :], ov[:, :, 1, :], ALU.add))
                link(dve.tensor_tensor(hp, hp, o2v, ALU.add))
                ln_stats(TJ * p, TJ * (p + 1))

            mish(0)
            image_tokens(0)
            dve.wait_ge(ld_txt, 16 * 3 * PAIRS)
            ln_stats(0, 6)
            ln_scale(0, 6)
            mish(1)
            split(1)
            split(3)
            take_v(0)
            image_tokens(1)
            ln_stats(6, 12)
            ln_scale(6, 12)
            take_v(1)
            for a in range(TJ * HEADS):
                row_max(0, a // TJ, a % TJ)
                if (a + 1) % GH == 0:
                    split_max(0, a // GH)
            for p in range(PAIRS):
                nxt = [(p + 1, a // TJ, a % TJ) for a in range(TJ * HEADS)] if p + 1 < PAIRS else []
                for hd in range(HEADS):
                    for g in nxt[4 * hd:4 * hd + 4]:
                        row_max(*g)
                    if hd in (2, 5) and nxt:
                        split_max(p + 1, hd // 5)
                    if hd == 2 and p + 2 < PAIRS:
                        take_v(p + 2)
                    if hd == 0 and p == PAIRS - 1:
                        ln_scale(0, 6)
                    if hd == 5 and p >= 1:
                        out_tile(p - 1, 0)
                    if hd == 6 and p >= 1:
                        out_tile(p - 1, 1)
                        out_tile(p - 1, 2)
                        out_join(p - 1)
            ln_scale(6, 9)
            for j in range(TJ):
                out_tile(PAIRS - 1, j)
            out_join(PAIRS - 1)
            ln_scale(9, 12)

            dve.wait_ge(lg_mm, 1)
            link(dve.tensor_copy(lg[:, :, :], bank[RANK_BANK][:, 0:T * E].rearrange("p (t e) -> p t e", e=E)))
            link(dve.tensor_reduce(mxl[:, :], lg[:, :, :], AX.X, ALU.max))
            def wide(ap):
                return ap.rearrange("p (t a) -> p t a", a=1).to_broadcast([128, T, E])
            def over_tiles(ap):
                return ap.rearrange("p (a e) -> p a e", a=1).to_broadcast([128, T, E])
            link(dve.tensor_tensor(oh[:, :, :], lg[:, :, :], wide(mxl[:, :]), ALU.is_ge))
            link(dve.tensor_tensor(oh[:, :, :], oh[:, :, :], over_tiles(C("prio")), ALU.mult))
            link(dve.tensor_reduce(mxl[:, :], oh[:, :, :], AX.X, ALU.max))
            link(dve.tensor_tensor(oh[:, :, :], oh[:, :, :], wide(mxl[:, :]), ALU.is_equal))
            dve.tensor_copy(oh_b[:, :, :], oh[:, :, :]).then_inc(oh_done, 1)
            dve.wait_ge(rank_mm, 1)
            link(dve.tensor_reduce(cnt[:, :], bank[RANK_BANK][:, 256:256 + T * E].rearrange("p (t e) -> p e t", e=E), AX.X, ALU.add))
            link(dve.tensor_scalar(cnt_i[:, :], cnt[:, :], 127.0, None, ALU.add))
            link(dve.tensor_scalar(cnt_i[:, :], cnt_i[:, :], 7, None, ALU.arith_shift_right))
            link(dve.tensor_copy(tiles_e[:, :], cnt_i[:, :]))
            link(dve.tensor_tensor_scan(incl[:, :], one8[:, :], tiles_e[:, :], 0.0, ALU.mult, ALU.add))
            link(dve.tensor_tensor(base[:, :], incl[:, :], tiles_e[:, :], ALU.subtract))
            link(dve.scalar_tensor_tensor(lg[:, :, :], over_tiles(base[:, :]), 128.0, bank[RANK_BANK][:, 128:128 + T * E].rearrange("p (t e) -> p t e", e=E),
                                          ALU.mult, ALU.add))
            link(dve.tensor_tensor(lg[:, :, :], lg[:, :, :], oh[:, :, :], ALU.mult))
            link(dve.tensor_reduce(slot_f[:, :], lg[:, :, :], AX.X, ALU.add))
            dve.tensor_copy(slot_u[:, :], slot_f[:, :]).then_inc(slot_done, 1)
            link(dve.tensor_tensor(cmp[:, :, :], incl[:, :].rearrange("p (a e) -> p a e", a=1).to_broadcast([128, SLOT_TILES, E]),
                                   C("tile_no").rearrange("p (t a) -> p t a", a=1).to_broadcast([128, SLOT_TILES, E]), ALU.is_le))
            link(dve.tensor_reduce(et_f[:, :], cmp[:, :, :], AX.X, ALU.add))
            link(dve.tensor_scalar(et_f[:, :], et_f[:, :], E - 1.0, None, ALU.min))
            dve.tensor_copy(et_i[:, :], et_f[:, :]).then_inc(et_done, 1)
            dve.memset(y_base[:, :, :], 0.0).then_inc(base_clear, 1)

            for tc in range(3):
                dve.wait_ge(sh_y, tc + 1)
                hv4 = h[:, 4 * tc:4 * tc + 4, :].rearrange("p t d -> p (t d)")
                dve.tensor_tensor(hv4, bank[SY_BANKS[tc]][:, :], hv4, ALU.add).then_inc(sh_add, 1)

            def take_x(t):
                dve.wait_ge(xs_ld[t % NX], 16 * (t // NX + 1))
                dve.tensor_copy(id_u[:, t:t + 1], xs[:, t % NX, D:XW]).then_inc(id_done, 1)
                dve.wait_ge(x_tr, t + 1)
                if t >= 2:
                    dve.wait_ge(up_b, t - 1)
                dve.tensor_copy(xsT[:, t % 2, :], bank[XT_BANK][:, 0:D]).then_inc(x_cp, 1)

            def gate(t):
                dve.wait_ge(up_b, t + 1)
                dve.wait_ge(silu_done, t + 1)
                if t >= 2:
                    dve.wait_ge(g_tr, t - 1)
                dve.tensor_tensor(gate_sb[:, t % 2, :], bank[UP_BANKS[1][t % 2]][:, :], sA[:, t % 2, :], ALU.mult).then_inc(gated, 1)

            def add_base(t):
                dve.wait_ge(y_mm, t + 1)
                dve.wait_ge(based[t % NY], 16 * (t // NY + 1))
                if t >= NY:
                    dve.wait_ge(stored[t % NY], 16 * (t // NY))
                dve.tensor_tensor(y_sb[:, t % NY, :], bank[Y_BANKS[t % 2]][:, 0:D], y_base[:, t % NY, :], ALU.add).then_inc(y_cp, 1)

            take_x(0)
            for t in range(SLOT_TILES):
                gate(t)
                if t + 1 < SLOT_TILES:
                    take_x(t + 1)
                if t >= 1:
                    add_base(t - 1)
            add_base(SLOT_TILES - 1)

        @block.tensor
        def _(pe):
            pe.wait_ge(ld_c, 16)
            pe.wait_ge(diag_done, 2)
            for m in range(2):
                ins = pe.matmul(bank[6][:, 128 * m:128 * (m + 1)], C("ones"), diag[:, m, :], start=True, stop=True)
            ins.then_inc(eo_mm, 1)
            pe.wait_ge(ld_x, 16)
            for half in range(2):
                for m, wsrc in enumerate((w1n, w2n)):
                    pe.wait_ge(noisy, m + 1)
                    for kc in range(KC):
                        ins = pe.matmul(bank[3 * half + m][:, 0:HALF_TOK], wsrc[:, kc, :], x_sb[:, kc, HALF_TOK * half:HALF_TOK * (half + 1)],
                                        start=(kc == 0), stop=(kc == KC - 1))
                    ins.then_inc(tok_mm, 1)

            def image_tokens(half):
                pe.wait_ge(act_done, half + 1)
                pe.wait_ge(ld_wp, 16)
                for b in range(B // 2):
                    p, odd = divmod(b, 2)
                    at = HALF_TOK * half + N_IMG * b
                    ins = pe.matmul(bank[2 + 3 * half][64 * odd:64 * odd + 64, D * p:D * (p + 1)], g_sb[:, at:at + N_IMG], W("w3"), start=True, stop=True)
                ins.then_inc(h_mm, 1)

            def transposes(n):
                pe.wait_ge(hn_ready, TJ * (n + 1))
                if n >= 2:
                    pe.wait_ge(hnT_done, n - 1)
                if n >= PAIRS and n < PAIRS + 2:
                    pe.wait_ge(s_max, TJ * HEADS * PAIRS)
                for i in range(TJ):
                    ins = pe.transpose(bank[n % 2][:, 128 * i:128 * (i + 1)], hn[:, TJ * (n % PAIRS) + i, 0:D], ident)
                ins.then_inc(tr_done, 1)

            image_tokens(0)

            def wait_bank(item):
                n = misc_no[item]
                if n >= 2:
                    pe.wait_ge(*evacuated(misc_order[n - 2]))

            def proj(p, n):
                tok = slice(PT * p, PT * (p + 1))
                pe.wait_ge(hnT_done, p + 1)
                item = ("proj", p, n)
                wait_bank(item)
                if n < 4:
                    w = W("wk" if n % 2 else "wq")[:, 128 * (n // 2):128 * (n // 2) + 128]
                    pe.matmul(mbank(item)[:, 0:PT], w, hnT[:, tok], start=True, stop=True).then_inc(misc_ready, 1)
                    return
                for j in range(TJ):
                    ins = pe.matmul(mbank(item)[:, 128 * j:128 * (j + 1)], hnT[:, PT * p + 128 * j:PT * p + 128 * (j + 1)], W("wv"), start=True, stop=True)
                ins.then_inc(misc_ready, 1)

            def score(p, hd, j):
                g = TJ * (HEADS * p + hd) + j
                if g == 0:
                    pe.wait_ge(hnT_done, PAIRS)
                if g % GH == 0:
                    pe.wait_ge(stack_ld[p % NST][hd // 4], 16 * 6 * (p // NST + 1))
                if g >= 2:
                    pe.wait_ge(s_max, g - 1)
                for s in range(2):
                    for r0, rn, bb in batches(j):
                        ins = pe.matmul(bank[g % 2][r0:r0 + rn, SEQ * s:SEQ * (s + 1)],
                                        q_st[p % NST][0:SROWS, 2 * hd + s, 128 * j + r0:128 * j + r0 + rn],
                                        k_st[p % NST][0:SROWS, 2 * hd + s, SEQ * bb:SEQ * (bb + 1)], start=True, stop=True)
                ins.then_inc(s_ready, 1)

            def max_rows(p, ch):
                item = ("max", p, ch)
                pe.wait_ge(init_done, INIT)
                pe.wait_ge(mx_split, 2 * p + ch + 1)
                wait_bank(item)
                for j in range(TJ):
                    ins = pe.matmul(mbank(item)[0:NPART * HSC, 128 * j:128 * (j + 1)], mx_s[:, ch, j, :, :].rearrange("p s g -> p (s g)"), ident_b[:, :],
                                    start=True, stop=True)
                ins.then_inc(misc_ready, 1)

            def score_t(p, hd, j):
                g = TJ * (HEADS * p + hd) + j
                if g % GH == 0:
                    pe.wait_ge(max_ld[p % NST][hd // 4], 16 * NPART * (p // NST + 1))
                    pe.wait_ge(ones_done, NST)
                if g >= 2:
                    pe.wait_ge(exp_done, g - 1)
                for s in range(2):
                    for r0, rn, bb in batches(j):
                        ins = pe.matmul(bank[2 + g % 2][r0:r0 + rn, SEQ * s:SEQ * (s + 1)],
                                        k_st[p % NST][0:SROWS + NPART, 2 * hd + s, 128 * j + r0:128 * j + r0 + rn],
                                        q_st[p % NST][0:SROWS + NPART, 2 * hd + s, SEQ * bb:SEQ * (bb + 1)], start=True, stop=True)
                ins.then_inc(st_ready, 1)

            def weigh(half, u):
                bb, i = divmod(u, 2)
                j, r0, rn = (((0, 0, 128), (1, 0, SHALF)), ((1, SHALF, 128 - SHALF), (2, 0, 128)))[bb][i]
                p, hg = divmod(half, 2)
                if u == 0:
                    pe.wait_ge(exp_done, GH * (half + 1))
                    pe.wait_ge(v_done, p + 1)
                if i == 0 and half >= 1:
                    pe.wait_ge(av_free[bb], half)
                for a in range(4):
                    ins = pe.matmul(bank[4 + bb][32 * a:32 * a + 32, 0:2 * SEQ], vaug[r0:r0 + rn, TJ * p + j, 4 * hg + a, :],
                                    p_ring[r0:r0 + rn, half % 2, TJ * a + j, :, :].rearrange("p s q -> p (s q)"), start=(i == 0), stop=(i == 1))
                ins.then_inc(av_done, 1)

            def out_rows(p, j):
                for bb in range(2):
                    pe.wait_ge(av_free[bb], 2 * (p + 1))
                item = ("out", p, j)
                wait_bank(item)
                for hg in range(2):
                    for s in range(2):
                        c = 128 * (2 * hg + s)
                        ins = pe.transpose(mbank(item)[:, c:c + 128], oT[:, hg, s, 128 * j:128 * (j + 1)], ident)
                ins.then_inc(misc_ready, 1)

            transposes(0)
            for n in range(5):
                proj(0, n)
            image_tokens(1)
            transposes(1)
            for n in range(5):
                proj(1, n)
            transposes(2)
            transposes(3)
            for g in range(TJ * HEADS):
                if g == GH + 3:
                    max_rows(0, 0)
                score(0, g // TJ, g % TJ)
            for p in range(PAIRS):
                nxt = [(p + 1, a // TJ, a % TJ) for a in range(TJ * HEADS)] if p + 1 < PAIRS else []
                for hd in range(HEADS):
                    half = 2 * p + hd // 4
                    ahead = nxt[4 * hd:4 * hd + 4]
                    for j in range(TJ):
                        if ahead:
                            score(*ahead[j])
                        score_t(p, hd, j)
                        if (p, hd, j) == (0, 0, 0):
                            max_rows(0, 1)
                        if j == 0:
                            if hd == 6 and nxt:
                                max_rows(p + 1, 1)
                        if j == 1:
                            if hd < 3 and p + 2 < PAIRS:
                                proj(p + 2, 2 * hd)
                            if hd == 3 and nxt:
                                max_rows(p + 1, 0)
                            if hd == 6 and p >= 1:
                                out_rows(p - 1, 1)
                            if hd in (3, 4) and p == PAIRS - 1:
                                transposes(PAIRS + hd - 3)
                    if ahead:
                        score(*ahead[3])
                    if half >= 1:
                        weigh(half - 1, hd % 4)
                    if hd < 2 and p + 2 < PAIRS:
                        proj(p + 2, 2 * hd + 1)
                    if hd in (5, 6) and p >= 1:
                        out_rows(p - 1, 2 * (hd - 5))
            for u in range(4):
                weigh(2 * PAIRS - 1, u)

            def logits(t0, t1):
                pe.wait_ge(hnT_done, PAIRS + (t1 - 1) // TJ + 1)
                for t in range(t0, t1):
                    ins = pe.matmul(bank[RANK_BANK][:, E * t:E * (t + 1)], hnT[:, 128 * t:128 * (t + 1)], W("gate"), start=True, stop=True)
                if t1 == T:
                    ins.then_inc(lg_mm, 1)

            def sh_hidden(k):
                tc, ic = divmod(k, IC)
                pe.wait_ge(hnT_done, PAIRS + (4 * tc + 3) // TJ + 1)
                if k >= 4:
                    pe.wait_ge(sh_act, k - 3)
                elif k < 2:
                    pe.wait_ge(exp_done, TJ * HEADS * PAIRS)
                else:
                    pe.wait_ge(out_read, TJ * PAIRS)
                pe.matmul(bank[SH_BANKS[k % 4]][:, :], W("sw1")[:, 128 * ic:128 * (ic + 1)], hnT[:, 512 * tc:512 * (tc + 1)], start=True, stop=True)\
                    .then_inc(sh_mm, 1)

            def sh_out(tc):
                pe.wait_ge(sh_act, IC * (tc + 1))
                if tc == 0:
                    pe.wait_ge(av_free[1], 2 * PAIRS)
                if tc >= 2:
                    pe.wait_ge(sh_add, tc - 1)
                for i in range(4):
                    for ic in range(IC):
                        ins = pe.matmul(bank[SY_BANKS[tc]][:, 128 * i:128 * (i + 1)], a_sh[:, tc % 2, ic, 128 * i:128 * (i + 1)],
                                        W("sw2")[:, D * ic:D * (ic + 1)], start=(ic == 0), stop=(ic == IC - 1))
                ins.then_inc(sh_y, 1)

            for j in range(TJ):
                out_rows(PAIRS - 1, j)
            transposes(PAIRS + 2)
            logits(0, 9)
            for k in range(4):
                sh_hidden(k)
            transposes(PAIRS + 3)
            logits(9, T)
            sh_hidden(4)
            sh_hidden(5)
            pe.wait_ge(oh_done, 1)
            rank = bank[RANK_BANK][:, 128:128 + T * E]
            ohv = oh_b[:, :, :].rearrange("p t e -> p (t e)")
            pe.matmul(rank, tri_b[:, :], ohv, start=True, stop=False)
            for u in range(1, T):
                pe.matmul(rank[:, E * u:T * E], ones_b[:, :], ohv[:, 0:E * (T - u)], start=False, stop=(u == T - 1))
            pe.matmul(bank[RANK_BANK][:, 256:256 + T * E], ones_b[:, :], ohv, start=True, stop=True).then_inc(rank_mm, 1)
            sh_out(0)
            for k in range(6, 12):
                sh_hidden(k)
            sh_out(1)
            sh_out(2)

            def turn_x(t):
                pe.wait_ge(xs_ld[t % NX], 16 * (t // NX + 1))
                if t >= 1:
                    pe.wait_ge(x_cp, t)
                else:
                    pe.wait_ge(slot_done, 1)
                pe.transpose(bank[XT_BANK][:, 0:D], xs[:, t % NX, 0:D], ident).then_inc(x_tr, 1)

            def up(t, e, m):
                pe.wait_ge(x_cp, t + 1)
                if m == 0 and t >= 2:
                    pe.wait_ge(silu_done, t - 1)
                if m == 1 and t >= 2:
                    pe.wait_ge(gated, t - 1)
                pe.matmul(bank[UP_BANKS[m][t % 2]][:, :], xsT[:, t % 2, :], w13_sb[:, bass.ds(e, 1), m, :].rearrange("p a i -> p (a i)"), start=True, stop=True)\
                    .then_inc(up_b if m else up_a, 1)

            def turn_g(t):
                pe.wait_ge(gated, t + 1)
                if t >= 1:
                    pe.wait_ge(g_cp, t)
                for c in range(IC):
                    ins = pe.transpose(bank[GT_BANK][:, 128 * c:128 * (c + 1)], gate_sb[:, t % 2, 128 * c:128 * (c + 1)], ident)
                ins.then_inc(g_tr, 1)

            def down(t, e):
                pe.wait_ge(g_cp, t + 1)
                if t >= 2:
                    pe.wait_ge(y_cp, t - 1)
                elif t == 0:
                    pe.wait_ge(sh_add, 3)
                for c in range(IC):
                    ins = pe.matmul(bank[Y_BANKS[t % 2]][:, 0:D], gT[:, t % 2, 128 * c:128 * (c + 1)],
                                    w2_sb[:, bass.ds(e, 1), c, :].rearrange("p a d -> p (a d)"), start=(c == 0), stop=(c == IC - 1))
                ins.then_inc(y_mm, 1)

            def expert_of(t):
                return pe.value_load(et_i[0:1, t:t + 1], min_val=0, max_val=E - 1)

            pe.wait_ge(ld_exp, 16 * 2 * E)
            pe.wait_ge(et_done, 1)
            pe.wait_ge(sh_act, 3 * IC)
            turn_x(0)
            e, prev = expert_of(0), None
            for t in range(SLOT_TILES):
                up(t, e, 0)
                if t >= 1:
                    turn_g(t - 1)
                up(t, e, 1)
                nxt = expert_of(t + 1) if t + 1 < SLOT_TILES else None
                if t + 1 < SLOT_TILES:
                    turn_x(t + 1)
                if t >= 1:
                    down(t - 1, prev)
                e, prev = nxt, e
            turn_g(SLOT_TILES - 1)
            down(SLOT_TILES - 1, prev)


def layouts(inputs):
    a = {k: np.ascontiguousarray(v) for k, v in inputs.items()}
    g = lambda n: a["L0_" + n]
    f32 = np.float32
    x = a["x"].reshape(B, SIDE, PATCH, SIDE, PATCH).transpose(2, 4, 0, 1, 3).reshape(KC, 128, B * N_IMG).transpose(1, 0, 2)
    wn = np.stack([g("tok_" + n).T.reshape(KC, 128, 128).transpose(1, 0, 2) for n in ("W1_w", "W1_sw", "W2_w", "W2_sw")], axis=1)

    def heads(w):
        return w.reshape(-1, 2, HSC, DH).transpose(0, 1, 3, 2).reshape(-1, 2 * D)

    col = lambda v: v.reshape(-1, 128).T
    n = dict(ei1=col(g("tok_eps_in1")), ei2=col(g("tok_eps_in2")), eo1=col(g("tok_eps_out1")), eo2=col(g("tok_eps_out2")),
             b1=col(g("tok_W1_b")), sb1=col(g("tok_W1_sb")), b2=col(g("tok_W2_b")), sb2=col(g("tok_W2_sb")),
             bq=col(heads(g("attn_bq"))), bk=col(heads(g("attn_bk"))))
    npack = np.concatenate([n[k] for k in N_COLS], axis=1)
    rows = np.stack([g("tok_W3_b"), g("attn_bv")])[None]
    w = dict(wq=heads(g("attn_Wq")), wk=heads(g("attn_Wk")), wv=g("attn_Wv"), w3=g("tok_W3_w").T, sw1=g("ffn_sw1").T,
             sw2=g("ffn_sw2").T.reshape(IC, 128, D).transpose(1, 0, 2).reshape(128, IC * D), gate=g("ffn_gate_w").T)
    wpack = np.concatenate([w[k] for k in W_COLS], axis=1)
    w13 = np.stack([g("ffn_w1").transpose(0, 2, 1), g("ffn_w3").transpose(0, 2, 1)], axis=2)
    w2 = g("ffn_w2").transpose(0, 2, 1).reshape(E, IC, 128, D).transpose(0, 2, 1, 3)
    pos = np.arange(N_IMG, dtype=f32)[:, None]
    div = np.exp(np.arange(0, D, 2, dtype=f32) * f32(-math.log(10000.0) / D))
    ang = pos * div
    pe = np.stack([np.sin(ang), np.cos(ang)], axis=-1).reshape(N_IMG, D).astype(f32)
    c = dict(token=np.arange(B * SEQ, dtype=f32).reshape(T, 128).T, ident=np.eye(128, dtype=f32), tri=np.triu(np.ones((128, 128), f32), 1), ones=np.ones((128, 128), f32),
             pe=np.concatenate([pe, pe]), tile_no=np.tile(np.arange(SLOT_TILES, dtype=f32), (128, 1)),
             prio=np.tile(np.arange(E, 0, -1).astype(f32), (128, 1)))
    cpack = np.concatenate([c[k] for k in C_COLS], axis=1)
    return {k: np.ascontiguousarray(v) for k, v in dict(xT=x, txt=a["txt"], wn=wn, npack=npack, rows=rows, wpack=wpack,
                                                        cpack=cpack, w13=w13, w2=w2).items()}


def kernel(**inputs):
    import concourse.bacc as bacc
    from concourse.bass_utils import run_bass_kernel_spmd

    nc = bacc.Bacc("TRN2", target_bir_lowering=False, num_devices=1)
    arrays, args = {}, []
    for name, a in layouts(inputs).items():
        arrays[f"in_{name}_dram"] = a
        args.append(nc.dram_tensor(f"in_{name}_dram", a.shape, mybir.dt.from_np(a.dtype), kind="ExternalInput").ap())
    o = nc.dram_tensor("out_dram", (B * SEQ, D), mybir.dt.float32, kind="ExternalOutput").ap()
    build_kernel(nc, *args, o)
    r = run_bass_kernel_spmd(nc, [arrays], core_ids=[0])
    return r.results[0]["out_dram"].reshape(B, SEQ, D)
```
